# Optimizing a Trainium2 kernel written in Bass

```python
import numpy as np
import jax
import jax.numpy as jnp

def _softmax(x, axis=-1):
    return jax.nn.softmax(x, axis=axis)

def _gelu(x):
    return jax.nn.gelu(x, approximate=True)

def _silu(x):
    return jax.nn.silu(x)

def _sigmoid(x):
    return jax.nn.sigmoid(x)

def _layernorm(x, axis=-1, eps=1e-05):
    m = jnp.mean(x, axis=axis, keepdims=True)
    v = jnp.var(x, axis=axis, keepdims=True)
    return (x - m) / jnp.sqrt(v + eps)

def _scatter_add(tgt, idx, src, axis=0):
    return tgt.at[idx].add(src)

def _segment_sum(src, seg, n):
    return jax.ops.segment_sum(src, seg, n)
kernel_name = 'mk_seq_preln_d1_jaxref_r8_da4def'

def setup_inputs(seed: int=0):
    np.random.seed(seed)
    _w = jnp.asarray

    def _L0_attn_setup():
        import jax, jax.numpy as jnp
        import numpy as np
        DIM = 128
        DIM_HEAD = 64
        HEADS = DIM // DIM_HEAD
        WINDOW = 32
        EPS = 1e-05

        def _rotate_half(x):
            x1, x2 = jnp.split(x, 2, axis=-1)
            return jnp.concatenate((-x2, x1), axis=-1)
        key = jax.random.key(seed)
        k0, k1, k2 = jax.random.split(key, 3)
        B, T = (2, 256)
        x = jax.random.normal(k0, (B, T, DIM), dtype=jnp.float32)
        ln_w = jnp.ones((DIM,), dtype=jnp.float32)
        ln_b = jnp.zeros((DIM,), dtype=jnp.float32)
        w_qkv = jax.random.normal(k1, (3 * DIM, DIM), dtype=jnp.float32) * (1.0 / np.sqrt(DIM))
        w_out = jax.random.normal(k2, (DIM, DIM), dtype=jnp.float32) * (1.0 / np.sqrt(DIM))
        return {'x': x, 'ln_w': ln_w, 'ln_b': ln_b, 'w_qkv': w_qkv, 'w_out': w_out}
    _L0_attn_in = _L0_attn_setup()

    def _L0_ffn_setup():
        import jax, jax.numpy as jnp
        import numpy as np
        E, H, I, K = (8, 128, 256, 2)
        B, S = (4, 256)
        key = jax.random.key(seed)
        k1, k2, k3, k4 = jax.random.split(key, 4)
        x = jax.random.normal(k1, (B, S, H), dtype=jnp.float32)
        router_w = jax.random.uniform(k2, (E, H), dtype=jnp.float32, minval=-1.0, maxval=1.0) / np.sqrt(H).astype(np.float32)
        w13 = jax.random.normal(k3, (E, H, 2 * I), dtype=jnp.float32) * 0.02
        w2 = jax.random.normal(k4, (E, I, H), dtype=jnp.float32) * 0.02
        return {'x': x, 'router_w': router_w, 'w13': w13, 'w2': w2}
    _L0_ffn_in = _L0_ffn_setup()
    _d = {'L0_attn_x': _L0_attn_in['x'], 'L0_attn_ln_w': _L0_attn_in['ln_w'], 'L0_attn_ln_b': _L0_attn_in['ln_b'], 'L0_attn_w_qkv': _L0_attn_in['w_qkv'], 'L0_attn_w_out': _L0_attn_in['w_out'], 'L0_ffn_router_w': _L0_ffn_in['router_w'], 'L0_ffn_w13': _L0_ffn_in['w13'], 'L0_ffn_w2': _L0_ffn_in['w2']}
    _x0 = _d['L0_attn_x']
    _d['L0_attn_x'] = jax.random.normal(jax.random.fold_in(jax.random.key(seed), 1), (4, 1024, 128), dtype=_x0.dtype)
    del _x0
    return _d

def reference(L0_attn_x, L0_attn_ln_w, L0_attn_ln_b, L0_attn_w_qkv, L0_attn_w_out, L0_ffn_router_w, L0_ffn_w13, L0_ffn_w2):

    def _L0_attn_ref(x, ln_w, ln_b, w_qkv, w_out):
        import jax, jax.numpy as jnp
        import numpy as np
        DIM = 128
        DIM_HEAD = 64
        HEADS = DIM // DIM_HEAD
        WINDOW = 32
        EPS = 1e-05

        def _rotate_half(x):
            x1, x2 = jnp.split(x, 2, axis=-1)
            return jnp.concatenate((-x2, x1), axis=-1)
        B, T, C = x.shape
        residual = x
        mu = jnp.mean(x, axis=-1, keepdims=True)
        var = jnp.mean(jnp.square(x - mu), axis=-1, keepdims=True)
        xn = (x - mu) * jax.lax.rsqrt(var + EPS) * ln_w + ln_b
        qkv = xn @ w_qkv.T
        q, k, v = jnp.split(qkv, 3, axis=-1)

        def to_heads(t):
            return t.reshape(B, T, HEADS, DIM_HEAD).transpose(0, 2, 1, 3)
        q, k, v = (to_heads(q), to_heads(k), to_heads(v))
        inv_freq = 1.0 / 10000.0 ** (jnp.arange(0, DIM_HEAD, 2, dtype=jnp.float32) / DIM_HEAD)
        t_pos = jnp.arange(T, dtype=jnp.float32)
        freqs = t_pos[:, None] * inv_freq[None, :]
        freqs = jnp.concatenate((freqs, freqs), axis=-1)
        cos, sin = (jnp.cos(freqs), jnp.sin(freqs))
        q = q * cos + _rotate_half(q) * sin
        k = k * cos + _rotate_half(k) * sin
        pos = jnp.arange(T)
        mask = (pos[:, None] >= pos[None, :]) & (pos[:, None] - pos[None, :] < WINDOW)
        scale = 1.0 / np.sqrt(DIM_HEAD)
        scores = jnp.einsum('bhqd,bhkd->bhqk', q, k) * scale
        scores = jnp.where(mask, scores, jnp.float32(-1e+30))
        attn = jax.nn.softmax(scores, axis=-1)
        out = jnp.einsum('bhqk,bhkd->bhqd', attn, v)
        out = out.transpose(0, 2, 1, 3).reshape(B, T, C) @ w_out.T
        return out + residual

    def _L0_ffn_ref(x, router_w, w13, w2):
        import jax, jax.numpy as jnp
        import numpy as np
        E, H, I, K = (8, 128, 256, 2)
        B, S = (4, 256)
        logits = jnp.einsum('bsh,eh->bse', x, router_w)
        probs = jax.nn.softmax(logits, axis=-1)
        weights, indices = jax.lax.top_k(probs, K)
        weights = weights / (weights.sum(axis=-1, keepdims=True) + 1e-06)
        h13 = jnp.einsum('bsh,ehi->bsei', x, w13)
        gate, up = jnp.split(h13, 2, axis=-1)
        h = jax.nn.silu(gate) * up
        y = jnp.einsum('bsei,eih->bseh', h, w2)
        y_sel = jnp.take_along_axis(y, indices[..., None], axis=2)
        return (y_sel * weights[..., None]).sum(axis=2)
    x = L0_attn_x
    x = x + _L0_attn_ref(_layernorm(x, axis=-1), L0_attn_ln_w, L0_attn_ln_b, L0_attn_w_qkv, L0_attn_w_out)
    x = x + _L0_ffn_ref(_layernorm(x, axis=-1), L0_ffn_router_w, L0_ffn_w13, L0_ffn_w2)
    return x

_drawn_inputs = setup_inputs


def setup_inputs(seed=0):
    import zlib

    import numpy as np

    out = dict(_drawn_inputs(seed))
    spreads = {'L0_attn_ln_w': (1.0, 0.2), 'L0_attn_ln_b': (0.0, 0.1)}
    factors = {'L0_ffn_router_w': 8.0, 'L0_ffn_w13': 8.0, 'L0_ffn_w2': 8.0}
    for name, (base, spread) in spreads.items():
        noise = np.random.default_rng([zlib.crc32(name.encode()), seed]).standard_normal(out[name].shape)
        drawn = base * np.exp(spread * noise) if base else spread * noise
        out[name] = jnp.asarray(drawn.astype(out[name].dtype))
    for name, factor in factors.items():
        out[name] = (out[name] * factor).astype(out[name].dtype)
    return out
```

```python
import numpy as np
import concourse.bass as bass
from concourse import mybir
from contextlib import ExitStack

BATCH, SEQ, DIM = 4, 1024, 128
HEADS, HEAD, BLOCK = 2, 64, 32
EXPERTS, HIDDEN = 8, 256
P = 128
HALF = 512
TPH = HALF // P
TPB = SEQ // P
HALVES = BATCH * SEQ // HALF
TOKENS = BATCH * SEQ
REGION = TOKENS + P
MOE_TILES = 2 * TOKENS // P + EXPERTS - 1
ROW = DIM + 2
NOWHERE = 4 * TOKENS
CONSTS = 12 * 16
EPS = 1e-5
MASKED = -1e30


def program(nc, x, ln_w, ln_b, w_qkv_t, w_rot_t, w_out_t, router_t, w13, w2, cos, sin, ident_in,
            small_in, row_in, squares_in, out):
    F32, BF16, I32 = mybir.dt.float32, mybir.dt.bfloat16, mybir.dt.int32
    ACT, ALU, AX = mybir.ActivationFunctionType, mybir.AluOpType, mybir.AxisListType
    E = EXPERTS

    expert_rows = nc.dram_tensor("expert_rows", [E * REGION + P, ROW], F32).ap()
    results = nc.dram_tensor("results", [2 * TOKENS, DIM], F32).ap()

    ctx = ExitStack()
    with ctx:
        def sb(name, shape, dt=F32):
            return ctx.enter_context(nc.sbuf_tensor(name, shape, dt))

        def sem(name):
            return ctx.enter_context(nc.semaphore(name))

        ident = sb("ident", [P, P])
        squares = sb("squares", [P, 4 * P])
        squares_bf = sb("squares_bf", [P, 4, P], BF16)
        ident_bf = squares_bf[:, 0, :]
        before_bf = squares_bf[:, 1, :]
        ones_bf = squares_bf[:, 2, :]
        mask_bf = squares_bf[:, 3, :].rearrange("p (a c) -> p a c", a=2)
        small = sb("small", [P, 2 * E])
        rows = sb("rows", [1, E * E + MOE_TILES * E + MOE_TILES])
        lnw = sb("lnw", [P, 1])
        lnb = sb("lnb", [P, 1])
        w_qkv = sb("w_qkv", [P, 3 * DIM])
        w_rot = sb("w_rot", [P, 2 * DIM])
        w_o = sb("w_o", [P, DIM])
        w_r = sb("w_r", [P, E])
        w13_sb = sb("w13_sb", [P, E, 2 * HIDDEN])
        w2_sb = sb("w2_sb", [P, E, 2, DIM])
        cos_sb = sb("cos_sb", [P, SEQ])
        sin_sb = sb("sin_sb", [P, SEQ])
        pad_rows = sb("pad_rows", [P, ROW])
        minus_half = sb("minus_half", [P, TPB])

        x_t = sb("x_t", [P, TPB, DIM])
        stat1 = sb("stat1", [P, TPB, 6])
        mv1 = sb("mv1", [P, TPB, 2])
        co = sb("co", [P, 8, TPB])
        y_n = sb("y_n", [P, TPB, DIM])
        s_t = sb("s_t", [P, TPB, DIM])
        xn_t = sb("xn_t", [P, BLOCK + SEQ])
        q_t = sb("q_t", [P, SEQ])
        k_t = sb("k_t", [P, BLOCK + SEQ])
        rope = sb("rope", [P, 4, HALF])
        v_sb = sb("v_sb", [P, 2, 2, TPH, DIM])
        prob = sb("prob", [P, HEADS * TPH, 64])
        prob_t = sb("prob_t", [P, HEADS * TPH, 2, P])
        smax = sb("smax", [P, HEADS * TPH])
        ssum = sb("ssum", [P, HEADS * TPH])
        srec = sb("srec", [P, HEADS * TPH])
        o_sb = sb("o_sb", [P, TPH, DIM])
        o_t = sb("o_t", [P, HALF])
        x2 = sb("x2", [P, 2, TPH, DIM])
        x2_all = sb("x2_all", [P, TOKENS // P, DIM])
        stat2 = sb("stat2", [P, TPH, 6])
        mv2 = sb("mv2", [P, TPH, 2])
        ve2 = sb("ve2", [P, TPH])
        r2 = sb("r2", [P, TPH])
        rowbuf = sb("rowbuf", [P, 2, 2, TPH, ROW])
        x3_t = sb("x3_t", [P, HALF])
        slots = sb("slots", [P, 2, 2, TPH], I32)
        lg = sb("lg", [P, TPH, E])
        ex = sb("ex", [P, TPH, E])
        t8 = [sb(f"t8_{n}", [P, TPH, E]) for n in range(8)]
        t1 = [sb(f"t1_{n}", [P, TPH]) for n in range(10)]
        slot_f = sb("slot_f", [P, 2, TPH])
        chosen = sb("chosen", [P, TPH, E], BF16)
        run = sb("run", [P, E])

        tb = [sb(f"tb_{n}", [1, E]) for n in range(5)]
        tb_i = sb("tb_i", [1, 2, E], I32)
        tbe = sb("tbe", [1, E, E])
        tbj = [sb(f"tbj_{n}", [1, MOE_TILES, E]) for n in range(2)]
        tj = [sb(f"tj_{n}", [1, MOE_TILES]) for n in range(3)]
        pad_at = sb("pad_at", [1, E], I32)
        tile_row = sb("tile_row", [1, MOE_TILES], I32)
        tile_exp = sb("tile_exp", [1, MOE_TILES], I32)
        XB = 8
        xg = sb("xg", [P, XB, ROW])
        xg_t = sb("xg_t", [P, 2, P])
        gate = sb("gate", [P, 2, HIDDEN])
        hid = sb("hid", [P, 2, HIDDEN])
        hid_t = sb("hid_t", [P, 2, 2, P])
        y_sb = sb("y_sb", [P, XB, DIM])

        res = sb("res", [P, 2, TPB, 2, DIM])

        ps = ctx.enter_context(nc.psum_tensor("ps", [P, 8, 512], F32))

        names = """waited x2_free consts w_loaded x_loaded x_used ln1_var ln1_coef yn_ready s_ready xT_mm xT_ev q_mm k_mm
            q_read k_read rope_a q_ready k_ready v_mm v_ev sc_mm sc_max sc_sub sc_exp sc_sum sc_rec sc_tr o_mm
            o_norm oT_mm oT_ev ao_mm x2_ready ln2_var ln2_coef x3_ready x3T_mm x3T_ev lg_mm lg_sub
            lg_exp chosen_ready pos_mm slots_ready x2_stored0 x2_stored1 scattered ln_chain moe_chain
            pool_chain front_chain score_chain route_chain tables padded zeroed halo
            g_mm g_silu h_ready hT_mm hT_ev y_mm y_ev
            gT_mm gT_ev res_loaded0 res_loaded1
            sum_a summed out_stored chain_t pads_ready""".split()
        S = {n: sem(n) for n in names}
        x2_stored = [S["x2_stored0"], S["x2_stored1"]]
        xg_loaded = [sem(f"xg_loaded{n}") for n in range(XB)]
        y_stored = [sem(f"y_stored{n}") for n in range(XB)]
        res_loaded = [S["res_loaded0"], S["res_loaded1"]]

        def wait_apart(eng, semaphore, value):
            eng.wait_ge(semaphore, value)
            eng.sem_inc(S["waited"], 1)

        class Chain:
            def __init__(self, eng, name, per_turn):
                self.eng, self.sem, self.per, self.base, self.n = eng, S[name], per_turn, 0, 0

            def turn(self, i):
                assert self.n in (0, self.per), (self.n, self.per)
                self.base, self.n = self.per * i, 0

            def link(self, ins, apart=False):
                self.n += 1
                ins.then_inc(self.sem, 1)
                (wait_apart if apart else type(self.eng).wait_ge)(self.eng, self.sem, self.base + self.n)

        def run_halves(eng, front, step):
            front(0, 0)
            with eng.Fori(0, BATCH - 1) as c:
                i = c * 2
                step(i, 0, True)
                step(i + 1, 1, True)
            step(HALVES - 2, 0, True)
            step(HALVES - 1, 1, False)

        x_h = x.rearrange("b (t p) d -> b p t d", p=P)
        res_h = results.rearrange("(b t p k) d -> b p t k d", t=TPB, p=P, k=2)
        out_h = out.rearrange("b (t p) d -> b p t d", p=P)
        block = ctx.enter_context(nc.Block())

        @block.sync
        def _(sp):
            sp.dma_start(x_t[:], x_h[0]).then_inc(S["x_loaded"], 16)
            for dst, src in ((ident, ident_in), (small, small_in), (rows, row_in), (lnw, ln_w), (lnb, ln_b),
                             (w_qkv, w_qkv_t), (w_rot, w_rot_t), (w_o, w_out_t), (w_r, router_t),
                             (cos_sb, cos), (sin_sb, sin)):
                sp.dma_start(dst[:], src).then_inc(S["consts"], 16)
            sp.dma_start(squares[:], squares_in).then_inc(S["consts"], 16)
            sp.dma_start(w13_sb[:], w13.rearrange("e p n -> p e n")).then_inc(S["w_loaded"], 16)
            sp.dma_start(w2_sb[:], w2.rearrange("e (c p) n -> p e c n", p=P)).then_inc(S["w_loaded"], 16)

            def store_x2(i, h):
                sp.wait_ge(S["x2_ready"], i + 1)
                sp.dma_start(x2_all[:, bass.ds(i * TPH, TPH), :], x2[:, h]).then_inc(x2_stored[h], 16)
                sp.wait_ge(x2_stored[h], i // 2 * 16 + 16)
                sp.sem_inc(S["x2_free"], 1)

            def step(i, h, more):
                if h == 0 and not isinstance(i, int):
                    sp.wait_ge(S["x_used"], i // 2 + 1)
                    sp.dma_start(x_t[:], x_h[bass.ds(i // 2 + 1, 1)].rearrange("b p t d -> p (b t) d"))\
                        .then_inc(S["x_loaded"], 16)
                store_x2(i, h)

            run_halves(sp, lambda i, h: None, step)

            sp.wait_ge(S["tables"], 1)
            sp.wait_ge(S["pads_ready"], 3)
            sp.wait_ge(S["scattered"], HALVES * 2 * TPH * 16)
            for e in range(E):
                at = sp.value_load(pad_at[0:1, e:e + 1], min_val=e * REGION, max_val=e * REGION + TOKENS)
                sp.dma_start(expert_rows[bass.ds(at, P), :], pad_rows[:]).then_inc(S["padded"], 16)
            sp.dma_start(expert_rows[E * REGION:E * REGION + P, :], pad_rows[:]).then_inc(S["padded"], 16)
            sp.wait_ge(S["padded"], 16 * (E + 1))

            def load_rows(j, n):
                at = sp.value_load(tile_row[0:1, bass.ds(j, 1)], min_val=0, max_val=E * REGION)
                sp.dma_start(xg[:, n, :], expert_rows[bass.ds(at, P), :]).then_inc(xg_loaded[n], 16)

            for j in range(XB):
                load_rows(j, j)
            with sp.Fori(1, MOE_TILES // XB) as m:
                for n in range(XB):
                    sp.wait_ge(y_stored[n], m * 16)
                    load_rows(m * XB + n, n)
            for j in range(MOE_TILES // XB * XB, MOE_TILES):
                sp.wait_ge(y_stored[j % XB], j // XB * 16)
                load_rows(j, j % XB)

            for n in range(XB):
                sp.wait_ge(y_stored[n], 16 * len(range(n, MOE_TILES, XB)))
            for b in range(BATCH):
                if b >= 2:
                    sp.wait_ge(S["summed"], b - 1)
                sp.dma_start(res[:, b % 2], res_h[b]).then_inc(res_loaded[b % 2], 16)
                if b >= 1:
                    sp.wait_ge(S["summed"], b)
                    sp.dma_start(out_h[b - 1], x2_all[:, (b - 1) * TPB:b * TPB, :]).then_inc(S["out_stored"], 16)
            sp.wait_ge(S["summed"], BATCH)
            sp.dma_start(out_h[BATCH - 1], x2_all[:, (BATCH - 1) * TPB:, :]).then_inc(S["out_stored"], 16)
            sp.wait_ge(S["out_stored"], 16 * BATCH)

        @block.gpsimd
        def _(pool):
            pool.memset(minus_half[:], -0.5).then_inc(S["pool_chain"], 1)
            pool.memset(prob_t[:], 0.0).then_inc(S["zeroed"], 1)
            pool.memset(run[:], 0.0).then_inc(S["zeroed"], 1)
            for k in range(2):
                for h in range(2):
                    pool.iota(rowbuf[:, h, k, :, DIM:DIM + 1].bitcast(I32), pattern=[[2 * P, TPH], [0, 1]],
                              base=2 * (h * HALF) + k - 2 * SEQ, channel_multiplier=2).then_inc(S["pool_chain"], 1)
            pool.wait_ge(S["pool_chain"], 5)
            pool.memset(pad_rows[:, 0:DIM], 0.0).then_inc(S["pads_ready"], 1)
            pool.memset(pad_rows[:, DIM + 1:ROW], 0.0).then_inc(S["pads_ready"], 1)
            pool.iota(pad_rows[:, DIM:DIM + 1].bitcast(I32), pattern=[[0, 1]], base=NOWHERE,
                      channel_multiplier=0).then_inc(S["pads_ready"], 1)

            ln1 = Chain(pool, "ln_chain", 9)
            ln2 = Chain(pool, "moe_chain", 1)
            rt = Chain(pool, "chain_t", 2)

            def roots1(b):
                ln1.turn(b)
                var, mean = mv1[:, :, 1], mv1[:, :, 0]
                ve, r1, u, w, r, r12, a, bs = (co[:, n, :] for n in range(8))
                wait_apart(pool, S["ln1_var"], b + 1)
                ln1.link(pool.tensor_scalar(ve, var, EPS, None, ALU.add), apart=True)
                ln1.link(pool.tensor_tensor(r1, ve, minus_half[:], ALU.pow), apart=True)
                ln1.link(pool.tensor_tensor(u, var, r1, ALU.mult), apart=True)
                ln1.link(pool.tensor_tensor(w, u, r1, ALU.mult), apart=True)
                ln1.link(pool.tensor_scalar(u, w, EPS, None, ALU.add), apart=True)
                ln1.link(pool.tensor_tensor(r, u, minus_half[:], ALU.pow), apart=True)
                ln1.link(pool.tensor_tensor(r12, r, r1, ALU.mult), apart=True)
                ln1.link(pool.tensor_scalar(a, r1, 1.0, None, ALU.add), apart=True)
                ln1.link(pool.tensor_tensor(u, mean, r1, ALU.mult), apart=True)
                pool.tensor_scalar(bs, u, -1.0, None, ALU.mult).then_inc(S["ln1_coef"], 1)

            def step(i, h, more):
                ln2.turn(i)
                wait_apart(pool, S["ln2_var"], i + 1)
                ln2.link(pool.tensor_scalar(ve2[:], mv2[:, :, 1], EPS, None, ALU.add), apart=True)
                pool.tensor_tensor(r2[:], ve2[:], minus_half[:, 0:TPH], ALU.pow).then_inc(S["ln2_coef"], 1)
                if h == 0 and not isinstance(i, int):
                    roots1(i // 2 + 1)
                rt.turn(i)
                place = rowbuf[:, h, :, :, DIM:DIM + 1].bitcast(I32).rearrange("p k t o -> p (k t) o")
                rt.link(pool.tensor_scalar(place, place, 2.0 * SEQ, None, ALU.add), apart=True)
                wait_apart(pool, S["x3_ready"], i + 1)
                rt.link(pool.tensor_copy(rowbuf[:, h, 1, :, 0:DIM], rowbuf[:, h, 0, :, 0:DIM]), apart=True)
                wait_apart(pool, S["slots_ready"], i + 1)
                for k in range(2):
                    for t in range(TPH):
                        pool.indirect_dma_start(
                            expert_rows[:, :], bass.IndirectOffsetOnAxis(ap=slots[:, h, k, t:t + 1], axis=0),
                            rowbuf[:, h, k, t, :], None).then_inc(S["scattered"], 16)
                wait_apart(pool, S["scattered"], 2 * TPH * 16 * (i + 1))

            roots1(0)
            run_halves(pool, lambda i, h: None, step)

            def store(n):
                pool.indirect_dma_start(
                    results[:, :], bass.IndirectOffsetOnAxis(ap=xg[:, n, DIM:DIM + 1].bitcast(I32), axis=0),
                    y_sb[:, n, :], None, bounds_check=2 * TOKENS - 1, oob_is_err=False).then_inc(y_stored[n], 16)

            with pool.Fori(0, MOE_TILES // XB) as m:
                for n in range(XB):
                    wait_apart(pool, S["y_ev"], m * XB + n + 1)
                    store(n)
            for j in range(MOE_TILES // XB * XB, MOE_TILES):
                pool.wait_ge(S["y_ev"], j + 1)
                store(j % XB)

        @block.tensor
        def _(pe):
            mm, tr = pe.matmul, pe.transpose

            def project_front(i, h):
                c0 = BLOCK + h * HALF
                pe.wait_ge(S["yn_ready"], i + 1)
                for t in range(TPH):
                    last = tr(ps[:, 6, t * P:(t + 1) * P], y_n[:, h * TPH + t, :], ident[:])
                last.then_inc(S["xT_mm"], 1)
                pe.wait_ge(S["xT_ev"], i + 1)
                if not (isinstance(i, int) and i == 0):
                    pe.wait_ge(S["v_ev"], i)
                xt = xn_t[:, c0:c0 + HALF]
                mm(ps[:, 2, :], w_qkv[:, 0:DIM], xt, start=True, stop=True)
                mm(ps[:, 3, :], w_rot[:, 0:DIM], xt, start=True, stop=True).then_inc(S["q_mm"], 1)
                mm(ps[:, 4, :], w_qkv[:, DIM:2 * DIM], xt, start=True, stop=True)
                mm(ps[:, 5, :], w_rot[:, DIM:2 * DIM], xt, start=True, stop=True).then_inc(S["k_mm"], 1)

            def project_v(i, h):
                pe.wait_ge(S["q_read"], i + 1)
                for s in range(2):
                    for t in range(TPH):
                        at = (BLOCK if s == 0 else 0) + h * HALF + t * P
                        last = mm(ps[:, 2 + s, t * P:(t + 1) * P], xn_t[:, at:at + P], w_qkv[:, 2 * DIM:],
                                  start=True, stop=True)
                last.then_inc(S["v_mm"], 1)

            def scores(i, h):
                pe.wait_ge(S["q_ready"], i + 1)
                pe.wait_ge(S["k_ready"], i + 1)
                for a in range(HEADS):
                    first = 1 if h == 0 else 0
                    if first:
                        mm(ps[:, a, 0:64], ident_bf, mask_bf[:, 0, :], start=True, stop=True)
                    mm(ps[:, a, 64 * first:64 * TPH], ident_bf,
                       mask_bf[:, 1:2, :].to_broadcast([P, TPH - first, 64]), start=not first, stop=True,
                       skip_group_check=True)
                for t in range(TPH):
                    for g in range(P // BLOCK):
                        at = h * HALF + t * P + g * BLOCK
                        for a in range(HEADS):
                            last = mm(ps[g * BLOCK:(g + 1) * BLOCK, a, t * 64:(t + 1) * 64],
                                      q_t[a * HEAD:(a + 1) * HEAD, at:at + BLOCK],
                                      k_t[a * HEAD:(a + 1) * HEAD, at:at + 2 * BLOCK],
                                      start=False, stop=True, skip_group_check=True)
                last.then_inc(S["sc_mm"], 1)

            def values(i, h):
                pe.wait_ge(S["sc_tr"], i + 1)
                pe.wait_ge(S["v_ev"], i + 1)
                for t in range(TPH):
                    for a in range(HEADS):
                        o = ps[:, 6, t * P + a * HEAD:t * P + (a + 1) * HEAD]
                        mm(o, prob_t[:, a * TPH + t, 1, :], v_sb[:, h, 0, t, a * HEAD:(a + 1) * HEAD],
                           start=True, stop=False)
                        last = mm(o, prob_t[:, a * TPH + t, 0, :], v_sb[:, h, 1, t, a * HEAD:(a + 1) * HEAD],
                                  start=False, stop=True)
                last.then_inc(S["o_mm"], 1)

            def back(i, h):
                pe.wait_ge(S["o_norm"], i + 1)
                for t in range(TPH):
                    last = tr(ps[:, 7, t * P:(t + 1) * P], o_sb[:, t, :], ident[:])
                last.then_inc(S["oT_mm"], 1)
                pe.wait_ge(S["oT_ev"], i + 1)
                for t in range(TPH):
                    last = mm(ps[:, 0, t * P:(t + 1) * P], o_t[:, t * P:(t + 1) * P], w_o[:], start=True, stop=True)
                last.then_inc(S["ao_mm"], 1)
                pe.wait_ge(S["x3_ready"], i + 1)
                for t in range(TPH):
                    last = tr(ps[:, 6, t * P:(t + 1) * P], rowbuf[:, h, 0, t, 0:DIM], ident[:])
                last.then_inc(S["x3T_mm"], 1)
                pe.wait_ge(S["x3T_ev"], i + 1)
                for t in range(TPH):
                    last = mm(ps[:, 7, t * E:(t + 1) * E], x3_t[:, t * P:(t + 1) * P], w_r[:], start=True, stop=True)
                last.then_inc(S["lg_mm"], 1)
                pe.wait_ge(S["chosen_ready"], i + 1)
                ch = chosen[:].rearrange("p t e -> p (t e)")
                mm(ps[:, 7, 64:64 + TPH * E], before_bf, ch, start=True, stop=True, skip_group_check=True)
                for t in range(TPH - 1):
                    n = TPH - 1 - t
                    mm(ps[:, 7, 64 + (t + 1) * E:64 + TPH * E], ones_bf,
                       chosen[:, t:t + 1, :].to_broadcast([P, n, E]), start=False, stop=True,
                       skip_group_check=True)
                for t in range(TPH):
                    last = mm(ps[:, 7, 64 + TPH * E:64 + (TPH + 1) * E], ones_bf, chosen[:, t, :],
                              start=False, stop=True, skip_group_check=True)
                last.then_inc(S["pos_mm"], 1)

            def front(i, h):
                project_front(i, h)
                project_v(i, h)

            def step(i, h, more):
                if not (isinstance(i, int) and i == 0):
                    pass
                scores(i, h)
                if more:
                    project_front(i + 1, 1 - h)
                values(i, h)
                if more:
                    project_v(i + 1, 1 - h)
                back(i, h)

            pe.wait_ge(S["consts"], CONSTS)
            pe.wait_ge(S["halo"], 3)
            pe.wait_ge(S["zeroed"], 2)
            run_halves(pe, front, step)

            def rows_t(j, n, p):
                pe.wait_ge(xg_loaded[n], (j // XB + 1) * 16)
                tr(ps[:, 2 + p, 0:P], xg[:, n, 0:DIM], ident[:]).then_inc(S["gT_mm"], 1)

            def expert(j):
                return pe.value_load(tile_exp[0:1, bass.ds(j, 1)], min_val=0, max_val=E - 1)

            def hidden(j, p, e):
                pe.wait_ge(S["gT_ev"], j + 1)
                if not isinstance(j, int) or j >= 2:
                    pe.wait_ge(S["h_ready"], j - 1)
                mm(ps[:, p, :], xg_t[:, p, :], w13_sb[:, bass.ds(e, 1), :], start=True, stop=True)\
                    .then_inc(S["g_mm"], 1)

            def hidden_t(j, p):
                pe.wait_ge(S["h_ready"], j + 1)
                for c in range(2):
                    last = tr(ps[:, 4 + p, c * P:(c + 1) * P], hid[:, p, c * P:(c + 1) * P], ident[:])
                last.then_inc(S["hT_mm"], 1)

            def result(j, p, e):
                pe.wait_ge(S["hT_ev"], j + 1)
                if not isinstance(j, int) or j >= 2:
                    pe.wait_ge(S["y_ev"], j - 1)
                for c in range(2):
                    last = mm(ps[:, 6 + p, 0:DIM], hid_t[:, p, c, :], w2_sb[:, bass.ds(e, 1), c, :],
                              start=(c == 0), stop=(c == 1))
                last.then_inc(S["y_mm"], 1)

            pe.wait_ge(S["w_loaded"], 32)
            pe.wait_ge(S["tables"], 1)
            rows_t(0, 0, 0)
            rows_t(1, 1, 1)
            hidden(0, 0, expert(0))
            rows_t(2, 2, 0)
            hidden(1, 1, expert(1))
            hidden_t(0, 0)

            def tile_turn(j, n, p, loaded):
                if loaded is not None:
                    pe.wait_ge(xg_loaded[n], loaded * 16)
                    tr(ps[:, 3 - p, 0:P], xg[:, n, 0:DIM], ident[:]).then_inc(S["gT_mm"], 1)
                hidden(j, p, expert(j))
                hidden_t(j - 1, 1 - p)
                result(j - 2, p, expert(j - 2))

            def plain_turn(j):
                more = j + 1 < MOE_TILES
                tile_turn(j, (j + 1) % XB, j % 2, (j + 1) // XB + 1 if more else None)

            first = 2 + XB
            full = (MOE_TILES - first) // XB
            for j in range(2, first):
                plain_turn(j)
            with pe.Fori(0, full) as m:
                for n in range(XB):
                    tile_turn(m * XB + first + n, (first + n + 1) % XB, n % 2, m + (first + n + 1) // XB + 1)
            for j in range(first + full * XB, MOE_TILES):
                plain_turn(j)
            j = MOE_TILES
            hidden_t(j - 1, (j - 1) % 2)
            result(j - 2, j % 2, expert(j - 2))
            result(j - 1, (j - 1) % 2, expert(j - 1))

        @block.scalar
        def _(act):
            ac = act.activation

            def front_x(i, h):
                act.wait_ge(S["xT_mm"], i + 1)
                ac(xn_t[:, BLOCK + h * HALF:BLOCK + (h + 1) * HALF], ps[:, 6, :], ACT.Identity,
                   bias=lnb[:, 0:1], scale=lnw[:, 0:1]).then_inc(S["xT_ev"], 1)

            def front_v(i, h):
                act.wait_ge(S["v_mm"], i + 1)
                ac(v_sb[:, h].rearrange("p s t d -> p s (t d)"), ps[:, 2:4, :], ACT.Copy).then_inc(S["v_ev"], 1)

            def front(i, h):
                front_x(i, h)
                front_v(i, h)

            def step(i, h, more):
                if more:
                    front_x(i + 1, 1 - h)
                act.wait_ge(S["sc_sub"], i + 1)
                ac(prob[:], prob[:], ACT.Exp, scale=float(HEAD) ** -0.5).then_inc(S["sc_exp"], 1)
                if more:
                    front_v(i + 1, 1 - h)
                act.wait_ge(S["oT_mm"], i + 1)
                ac(o_t[:], ps[:, 7, :], ACT.Copy).then_inc(S["oT_ev"], 1)
                act.wait_ge(S["x3T_mm"], i + 1)
                ac(x3_t[:], ps[:, 6, :], ACT.Copy).then_inc(S["x3T_ev"], 1)
                act.wait_ge(S["lg_sub"], i + 1)
                ac(ex[:], lg[:], ACT.Exp).then_inc(S["lg_exp"], 1)

            act.wait_ge(S["consts"], CONSTS)
            ac(squares_bf[:].rearrange("p a c -> p (a c)"), squares[:], ACT.Copy).then_inc(S["halo"], 1)
            run_halves(act, front, step)

            def silu(j, p):
                act.wait_ge(S["g_mm"], j + 1)
                ac(gate[:, p, :], ps[:, p, 0:HIDDEN], ACT.Silu).then_inc(S["g_silu"], 1)

            def rows_ev(j, p):
                act.wait_ge(S["gT_mm"], j + 1)
                if not isinstance(j, int) or j >= 2:
                    act.wait_ge(S["g_mm"], j - 1)
                ac(xg_t[:, p, :], ps[:, 2 + p, 0:P], ACT.Copy).then_inc(S["gT_ev"], 1)

            rows_ev(0, 0)
            rows_ev(1, 1)
            silu(0, 0)
            with act.Fori(0, (MOE_TILES - 3) // 2) as m:
                for n in range(2):
                    j = m * 2 + 2 + n
                    rows_ev(j, n)
                    silu(j - 1, 1 - n)
            for j in range(2 + (MOE_TILES - 3) // 2 * 2, MOE_TILES):
                rows_ev(j, j % 2)
                silu(j - 1, (j - 1) % 2)
            silu(MOE_TILES - 1, (MOE_TILES - 1) % 2)

        @block.vector
        def _(dve):
            tt, ts, red = dve.tensor_tensor, dve.tensor_scalar, dve.tensor_reduce
            ln1 = Chain(dve, "front_chain", 1)
            route = Chain(dve, "route_chain", 26)
            sc = Chain(dve, "score_chain", 2)

            def stats(b):
                ln1.turn(b)
                dve.wait_ge(S["x_loaded"], 16 * b + 16)
                for t in range(TPB):
                    last = dve.bn_stats(stat1[:, t, :], x_t[:, t, :])
                ln1.link(last, apart=True)
                for t in range(TPB):
                    last = dve.bn_aggr(mv1[:, t, :], stat1[:, t, :])
                last.then_inc(S["ln1_var"], 1)

            def norm(i, h):
                b1 = i // 2 + 1
                dve.wait_ge(S["ln1_coef"], b1)
                for t in range(h * TPH, (h + 1) * TPH):
                    last = ts(y_n[:, t, :], x_t[:, t, :], mv1[:, t, 0:1], co[:, 5, t:t + 1], ALU.subtract, ALU.mult)
                last.then_inc(S["yn_ready"], 1)
                for t in range(h * TPH, (h + 1) * TPH):
                    last = ts(s_t[:, t, :], x_t[:, t, :], co[:, 6, t:t + 1], co[:, 7, t:t + 1], ALU.mult, ALU.add)
                if h == 1:
                    last.then_inc(S["x_used"], 1)
                    dve.wait_ge(S["x_used"], b1)

            def rotate(i, h):
                at = slice(h * HALF, (h + 1) * HALF)
                dve.wait_ge(S["q_mm"], i + 1)
                tt(rope[:, 0, :], ps[:, 2, :], cos_sb[:, at], ALU.mult)
                tt(rope[:, 1, :], ps[:, 3, :], sin_sb[:, at], ALU.mult).then_inc(S["q_read"], 1)
                dve.wait_ge(S["k_mm"], i + 1)
                tt(rope[:, 2, :], ps[:, 4, :], cos_sb[:, at], ALU.mult)
                tt(rope[:, 3, :], ps[:, 5, :], sin_sb[:, at], ALU.mult).then_inc(S["k_read"], 1)
                dve.wait_ge(S["q_read"], i + 1)
                tt(q_t[:, at], rope[:, 0, :], rope[:, 1, :], ALU.add).then_inc(S["q_ready"], 1)
                dve.wait_ge(S["k_read"], i + 1)
                tt(k_t[:, BLOCK + h * HALF:BLOCK + (h + 1) * HALF], rope[:, 2, :], rope[:, 3, :],
                   ALU.add).then_inc(S["k_ready"], 1)

            def softmax_a(i, h):
                sc.turn(i)
                s = ps[:, 0:2, 0:TPH * 64].rearrange("p a (t k) -> p a t k", k=64)
                dve.wait_ge(S["sc_mm"], i + 1)
                sc.link(red(smax[:], s, AX.X, ALU.max))
                for a in range(HEADS):
                    last = tt(prob[:, a * TPH:(a + 1) * TPH, :],
                              ps[:, a, 0:TPH * 64].rearrange("p (t k) -> p t k", k=64),
                              smax[:, a * TPH:(a + 1) * TPH].unsqueeze(2).to_broadcast([P, TPH, 64]), ALU.subtract)
                last.then_inc(S["sc_sub"], 1)

            def softmax_b(i, h):
                dve.wait_ge(S["sc_exp"], i + 1)
                for g in range(P // BLOCK):
                    q = slice(g * BLOCK, (g + 1) * BLOCK)
                    last = dve.transpose(prob_t[q, :, :, q].rearrange("p n s q -> p (n s) q"),
                                         prob[q].rearrange("p n (s k) -> p (n s) k", k=BLOCK))
                last.then_inc(S["sc_tr"], 1)
                sc.link(red(ssum[:], prob[:], AX.X, ALU.add))
                dve.reciprocal(srec[:], ssum[:]).then_inc(S["sc_rec"], 1)

            def attended(i, h):
                dve.wait_ge(S["o_mm"], i + 1)
                dve.wait_ge(S["sc_rec"], i + 1)
                tt(o_sb[:].rearrange("p t (a d) -> p t a d", d=HEAD),
                   ps[:, 6, :].rearrange("p (t a d) -> p t a d", a=HEADS, d=HEAD),
                   srec[:].rearrange("p (a t) -> p t a", t=TPH).unsqueeze(3).to_broadcast([P, TPH, HEADS, HEAD]),
                   ALU.mult).then_inc(S["o_norm"], 1)

            def second_norm(i, h):
                dve.wait_ge(S["ao_mm"], i + 1)
                dve.wait_ge(S["x2_free"], i + 1)
                tt(x2[:, h].rearrange("p t d -> p (t d)"), ps[:, 0, :],
                   s_t[:, h * TPH:(h + 1) * TPH, :].rearrange("p t d -> p (t d)"), ALU.add)\
                    .then_inc(S["x2_ready"], 1)
                dve.wait_ge(S["x2_ready"], i + 1)
                for t in range(TPH):
                    last = dve.bn_stats(stat2[:, t, :], x2[:, h, t, :])
                route.turn(i)
                route.link(last, apart=True)
                for t in range(TPH):
                    last = dve.bn_aggr(mv2[:, t, :], stat2[:, t, :])
                last.then_inc(S["ln2_var"], 1)
                dve.wait_ge(S["ln2_coef"], i + 1)
                for t in range(TPH):
                    last = ts(rowbuf[:, h, 0, t, 0:DIM], x2[:, h, t, :], mv2[:, t, 0:1], r2[:, t:t + 1],
                              ALU.subtract, ALU.mult)
                last.then_inc(S["x3_ready"], 1)

            def routing(i, h):
                lk = route.link
                per_e = lambda a: a.unsqueeze(2).to_broadcast([P, TPH, E])
                rank = small[:, 0:E].unsqueeze(1).to_broadcast([P, TPH, E])
                logit = ps[:, 7, 0:TPH * E].rearrange("p (t e) -> p t e", e=E)
                dve.wait_ge(S["lg_mm"], i + 1)
                lk(red(t1[0][:], logit, AX.X, ALU.max))
                tt(lg[:], logit, per_e(t1[0][:]), ALU.subtract).then_inc(S["lg_sub"], 1)
                dve.wait_ge(S["lg_exp"], i + 1)

                def pick(val, best, same, key, top, choice):
                    lk(red(best[:], val, AX.X, ALU.max))
                    lk(tt(same[:], val, per_e(best[:]), ALU.is_equal))
                    lk(tt(key[:], same[:], rank, ALU.mult))
                    lk(red(top[:], key[:], AX.X, ALU.max))
                    lk(tt(choice[:], key[:], per_e(top[:]), ALU.is_equal))

                first, second = t8[2], t8[5]
                pick(ex[:], t1[1], t8[0], t8[1], t1[2], first)
                lk(dve.scalar_tensor_tensor(out=t8[6][:], in0=first[:], scalar=-4.0, in1=ex[:],
                                            op0=ALU.mult, op1=ALU.add))
                pick(t8[6][:], t1[3], t8[3], t8[4], t1[4], second)
                tt(chosen[:], first[:], second[:], ALU.add).then_inc(S["chosen_ready"], 1)
                lk(red(t1[5][:], ex[:], AX.X, ALU.add))
                lk(dve.scalar_tensor_tensor(out=t1[6][:], in0=t1[5][:], scalar=1e-6, in1=t1[1][:],
                                            op0=ALU.mult, op1=ALU.add))
                lk(tt(t1[7][:], t1[6][:], t1[3][:], ALU.add))
                lk(dve.reciprocal(t1[8][:], t1[7][:]))
                for k, best in ((0, t1[1]), (1, t1[3])):
                    lk(tt(rowbuf[:, h, k, :, DIM + 1], best[:], t1[8][:], ALU.mult))
                lk(tt(t8[7][:, 0, :], run[:], small[:, E:2 * E], ALU.add))
                dve.wait_ge(S["pos_mm"], i + 1)
                lk(tt(t8[0][:], ps[:, 7, 64:64 + TPH * E].rearrange("p (t e) -> p t e", e=E),
                      t8[7][:, 0:1, :].to_broadcast([P, TPH, E]), ALU.add))
                lk(tt(run[:], ps[:, 7, 64 + TPH * E:64 + (TPH + 1) * E], run[:], ALU.add))
                for k, choice in ((0, first), (1, second)):
                    lk(tt(t8[1 + 2 * k][:], t8[0][:], choice[:], ALU.mult))
                    lk(red(slot_f[:, k, :], t8[1 + 2 * k][:], AX.X, ALU.add))
                dve.tensor_copy(slots[:, h], slot_f[:]).then_inc(S["slots_ready"], 1)

            def step(i, h, more):
                if more:
                    norm(i + 1, 1 - h)
                softmax_a(i, h)
                softmax_b(i, h)
                if more:
                    rotate(i + 1, 1 - h)
                attended(i, h)
                second_norm(i, h)
                if h == 0 and not isinstance(i, int):
                    stats(i // 2 + 1)
                routing(i, h)

            def front(i, h):
                norm(i, h)
                rotate(i, h)

            dve.sem_inc(S["x2_free"], 2)
            dve.memset(xn_t[:, 0:BLOCK], 0.0).then_inc(S["halo"], 1)
            dve.memset(k_t[:, 0:BLOCK], 0.0).then_inc(S["halo"], 1)
            stats(0)
            dve.wait_ge(S["consts"], CONSTS)
            dve.wait_ge(S["zeroed"], 2)
            run_halves(dve, front, step)

            ct = Chain(dve, "sum_a", 13)
            ct.turn(0)
            lk = ct.link
            le = rows[0:1, 0:E * E].rearrange("o (e f) -> o e f", f=E)
            jj = rows[0:1, E * E:E * E + MOE_TILES * E].rearrange("o (j e) -> o j e", e=E)
            j128 = rows[0:1, E * E + MOE_TILES * E:]
            lk(tt(tb[0][:], run[0:1, :], small[0:1, E:2 * E], ALU.add))
            lk(dve.tensor_copy(pad_at[:], tb[0][:]))
            lk(ts(tb_i[:, 0, :], run[0:1, :], float(P - 1), None, ALU.add))
            lk(ts(tb_i[:, 1, :], tb_i[:, 0, :], 7, None, ALU.arith_shift_right))
            lk(dve.tensor_copy(tb[1][:], tb_i[:, 1, :]))
            lk(tt(tbe[:], le, tb[1][:].unsqueeze(1).to_broadcast([1, E, E]), ALU.mult))
            lk(red(tb[2][:], tbe[:], AX.X, ALU.add))
            lk(ts(tb[3][:], tb[1][:], -float(P), float(REGION), ALU.mult, ALU.add))
            lk(tt(tbj[0][:], tb[2][:].unsqueeze(1).to_broadcast([1, MOE_TILES, E]), jj, ALU.is_le))
            lk(tt(tbj[1][:], tbj[0][:], tb[3][:].unsqueeze(1).to_broadcast([1, MOE_TILES, E]), ALU.mult))
            lk(red(tj[0][:], tbj[1][:], AX.X, ALU.add))
            lk(tt(tj[1][:], tj[0][:], j128, ALU.add))
            dve.tensor_scalar(tile_row[:], tj[1][:], float(E * REGION), None, ALU.min)
            lk(red(tj[2][:], tbj[0][:], AX.X, ALU.add))
            dve.tensor_scalar(tile_exp[:], tj[2][:], float(E - 1), None, ALU.min).then_inc(S["tables"], 1)

            def gated(j, p):
                dve.wait_ge(S["g_silu"], j + 1)
                if not isinstance(j, int) or j >= 2:
                    dve.wait_ge(S["hT_mm"], j - 1)
                tt(hid[:, p, :], ps[:, p, HIDDEN:2 * HIDDEN], gate[:, p, :], ALU.mult).then_inc(S["h_ready"], 1)

            def hidden_ev(j, p):
                dve.wait_ge(S["hT_mm"], j + 1)
                if not isinstance(j, int) or j >= 2:
                    dve.wait_ge(S["y_mm"], j - 1)
                dve.tensor_copy(hid_t[:, p].rearrange("p c q -> p (c q)"), ps[:, 4 + p, 0:2 * P])\
                    .then_inc(S["hT_ev"], 1)

            def result_ev(j, p, n, turn):
                dve.wait_ge(S["y_mm"], j + 1)
                if not isinstance(j, int) or j >= XB:
                    dve.wait_ge(y_stored[n], turn * 16)
                ts(y_sb[:, n, :], ps[:, 6 + p, 0:DIM], xg[:, n, DIM + 1:ROW], None, ALU.mult).then_inc(S["y_ev"], 1)

            def turn(j):
                gated(j, j % 2)
                if j >= 1:
                    hidden_ev(j - 1, (j - 1) % 2)
                if j >= 2:
                    result_ev(j - 2, j % 2, (j - 2) % XB, (j - 2) // XB)

            first = 2 + XB
            for j in range(first):
                turn(j)
            full = (MOE_TILES - first) // XB
            with dve.Fori(0, full) as m:
                for n in range(XB):
                    j = m * XB + first + n
                    gated(j, n % 2)
                    hidden_ev(j - 1, 1 - n % 2)
                    result_ev(j - 2, n % 2, n, m + 1)
            for j in range(first + full * XB, MOE_TILES):
                turn(j)
            j = MOE_TILES
            hidden_ev(j - 1, (j - 1) % 2)
            result_ev(j - 2, j % 2, (j - 2) % XB, (j - 2) // XB)
            result_ev(j - 1, (j - 1) % 2, (j - 1) % XB, (j - 1) // XB)

            dve.wait_ge(x2_stored[0], 16 * (HALVES // 2))
            dve.wait_ge(x2_stored[1], 16 * (HALVES // 2))
            for b in range(BATCH):
                dve.wait_ge(res_loaded[b % 2], 16 * (b // 2 + 1))
                tile = x2_all[:, b * TPB:(b + 1) * TPB, :]
                tt(tile, tile, res[:, b % 2, :, 0, :], ALU.add).then_inc(S["pads_ready"], 1)
                dve.wait_ge(S["pads_ready"], 3 + b + 1)
                tt(tile, tile, res[:, b % 2, :, 1, :], ALU.add).then_inc(S["summed"], 1)


def _tables():
    inv = (1.0 / np.float32(10000.0) ** (np.arange(0, HEAD, 2, dtype=np.float32) / np.float32(HEAD))).astype(np.float32)
    angle = (np.arange(SEQ, dtype=np.float32)[None, :] * inv[:, None]).astype(np.float32)
    cos = np.tile(np.cos(angle), (4, 1)).astype(np.float32)
    sin = np.sin(angle).astype(np.float32)
    sin = np.tile(np.concatenate([-sin, sin]), (2, 1)).astype(np.float32)
    k, m = np.arange(P)[:, None], np.arange(P)[None, :]
    q, key = np.arange(P)[:, None], np.arange(64)[None, :] - BLOCK
    dist = q % BLOCK - key
    seen = (dist >= 0) & (dist < BLOCK)
    start = seen & ((q >= BLOCK) | (key >= 0))
    mask = np.concatenate([np.where(s, 0.0, MASKED) for s in (start, seen)], axis=1)
    squares = np.concatenate([k == m, k < m, np.ones((P, P)), mask], axis=1).astype(np.float32)
    e = np.arange(EXPERTS)
    small = np.tile(np.concatenate([EXPERTS - e, e * REGION]).astype(np.float32), (P, 1))
    j = np.arange(MOE_TILES)
    row = np.concatenate([(e[None, :] <= e[:, None]).ravel(), np.repeat(j, EXPERTS), j * P]).astype(np.float32)
    return {"cos": cos, "sin": sin, "ident": (k == m).astype(np.float32), "small": small,
            "row": row[None, :], "squares": squares}


def kernel(L0_attn_x, L0_attn_ln_w, L0_attn_ln_b, L0_attn_w_qkv, L0_attn_w_out, L0_ffn_router_w,
           L0_ffn_w13, L0_ffn_w2):
    import concourse.bacc as bacc
    from concourse.bass_utils import run_bass_kernel_spmd

    qkv_t = np.asarray(L0_attn_w_qkv).T
    swap = np.arange(2 * DIM).reshape(-1, 2, HEAD // 2)[:, ::-1].ravel()
    arrays = {
        "x": L0_attn_x, "ln_w": np.asarray(L0_attn_ln_w)[:, None], "ln_b": np.asarray(L0_attn_ln_b)[:, None],
        "w_qkv_t": qkv_t, "w_rot_t": qkv_t[:, swap], "w_out_t": np.asarray(L0_attn_w_out).T,
        "router_t": np.asarray(L0_ffn_router_w).T, "w13": L0_ffn_w13, "w2": L0_ffn_w2, **_tables(),
    }
    arrays = {n: np.ascontiguousarray(a) for n, a in arrays.items()}
    nc = bacc.Bacc("TRN2", target_bir_lowering=False, num_devices=1)
    args = [nc.dram_tensor(f"in_{n}", a.shape, mybir.dt.from_np(a.dtype), kind="ExternalInput").ap()
            for n, a in arrays.items()]
    args.append(nc.dram_tensor("out", (BATCH, SEQ, DIM), mybir.dt.float32, kind="ExternalOutput").ap())
    program(nc, *args)
    r = run_bass_kernel_spmd(nc, [{f"in_{n}": a for n, a in arrays.items()}], core_ids=[0])
    return r.results[0]["out"]
```

```python
import numpy as np
import concourse.bass as bass
from concourse import mybir
from contextlib import ExitStack

BATCH, SEQ, DIM = 4, 1024, 128
HEADS, HEAD, BLOCK = 2, 64, 32
EXPERTS, HIDDEN = 8, 256
P = 128
HALF = 512
TPH = HALF // P
TPB = SEQ // P
HALVES = BATCH * SEQ // HALF
TOKENS = BATCH * SEQ
REGION = TOKENS + P
MOE_TILES = 2 * TOKENS // P + EXPERTS - 1
ROW = DIM + 2
NOWHERE = 4 * TOKENS
CONSTS = 13 * 16
EPS = 1e-5
MASKED = -1e30


def program(nc, x, ln_w, ln_b, w_qk_t, w_rot_t, w_v_in, w_out_t, router_t, w13, w2, cos, sin, ident_in,
            small_in, row_in, squares_in, out):
    F32, BF16, I32 = mybir.dt.float32, mybir.dt.bfloat16, mybir.dt.int32
    ACT, ALU, AX = mybir.ActivationFunctionType, mybir.AluOpType, mybir.AxisListType
    E = EXPERTS

    expert_rows = nc.dram_tensor("expert_rows", [E * REGION + P, ROW], F32).ap()
    results = nc.dram_tensor("results", [2 * TOKENS, DIM], F32).ap()

    ctx = ExitStack()
    with ctx:
        def sb(name, shape, dt=F32):
            return ctx.enter_context(nc.sbuf_tensor(name, shape, dt))

        def sem(name):
            return ctx.enter_context(nc.semaphore(name))

        ident = sb("ident", [P, P])
        squares = sb("squares", [P, 4 * P])
        squares_bf = sb("squares_bf", [P, 4, P], BF16)
        ident_bf = squares_bf[:, 0, :]
        before_bf = squares_bf[:, 1, :]
        ones_bf = squares_bf[:, 2, :]
        mask_bf = squares_bf[:, 3, :].rearrange("p (a c) -> p a c", a=2)
        small = sb("small", [P, 2 * E])
        rows = sb("rows", [1, E * E + MOE_TILES * E + MOE_TILES])
        lnw = sb("lnw", [P, 1])
        lnb = sb("lnb", [P, 1])
        w_qk = sb("w_qk", [P, 2 * DIM])
        w_v = sb("w_v", [P, DIM])
        w_vo = sb("w_vo", [P, HEADS, DIM])
        w_rot = sb("w_rot", [P, 2 * DIM])
        w_o = sb("w_o", [P, DIM])
        w_r = sb("w_r", [P, E])
        w13_sb = sb("w13_sb", [P, E, 2 * HIDDEN])
        w2_sb = sb("w2_sb", [P, E, 2, DIM])
        cos_sb = sb("cos_sb", [P, SEQ])
        sin_sb = sb("sin_sb", [P, SEQ])
        pad_rows = sb("pad_rows", [P, ROW])
        minus_half = sb("minus_half", [P, TPB])

        x_t = sb("x_t", [P, TPB, DIM])
        stat1 = sb("stat1", [P, TPB, 6])
        mv1 = sb("mv1", [P, TPB, 2])
        co = sb("co", [P, 8, TPB])
        var12, r12, var1, r1, m_r1, s_scale, s_bias = (co[:, n, :] for n in range(7))
        y_n = sb("y_n", [P, TPB, DIM])
        s_t = sb("s_t", [P, TPB, DIM])
        xn_t = sb("xn_t", [P, BLOCK + SEQ])
        q_t = sb("q_t", [P, SEQ])
        k_t = sb("k_t", [P, BLOCK + SEQ])
        rope = sb("rope", [P, 4, HALF])
        vo = sb("vo", [P, 2, TPH, HEADS, DIM])
        prob = sb("prob", [P, HEADS * TPH, 64])
        prob_t = sb("prob_t", [P, HEADS * TPH, 2, P])
        smax = sb("smax", [P, HEADS * TPH])
        ssum = sb("ssum", [P, HEADS * TPH])
        srec = sb("srec", [P, HEADS * TPH])
        x2 = sb("x2", [P, 2, TPH, DIM])
        x2_all = sb("x2_all", [P, TOKENS // P, DIM])
        stat2 = sb("stat2", [P, TPH, 6])
        mv2 = sb("mv2", [P, TPH, 2])
        ve2 = sb("ve2", [P, TPH])
        r2 = sb("r2", [P, TPH])
        rowbuf = sb("rowbuf", [P, 2, 2, TPH, ROW])
        x3_t = sb("x3_t", [P, HALF])
        slots = sb("slots", [P, 2, 2, TPH], I32)
        lg = sb("lg", [P, TPH, E])
        ex = sb("ex", [P, TPH, E])
        t8 = [sb(f"t8_{n}", [P, TPH, E]) for n in range(8)]
        t1 = [sb(f"t1_{n}", [P, TPH]) for n in range(10)]
        base = sb("base", [P, E])
        slot_f = sb("slot_f", [P, 2, TPH])
        chosen = sb("chosen", [P, TPH, E], BF16)
        run = sb("run", [P, E])

        tb = [sb(f"tb_{n}", [1, E]) for n in range(5)]
        tb_i = sb("tb_i", [1, 2, E], I32)
        tbe = sb("tbe", [1, E, E])
        tbj = [sb(f"tbj_{n}", [1, MOE_TILES, E]) for n in range(2)]
        tj = [sb(f"tj_{n}", [1, MOE_TILES]) for n in range(3)]
        pad_at = sb("pad_at", [1, E], I32)
        tile_row = sb("tile_row", [1, MOE_TILES], I32)
        tile_exp = sb("tile_exp", [1, MOE_TILES], I32)
        XB = 8
        xg = sb("xg", [P, XB, ROW])
        xg_t = sb("xg_t", [P, 2, P])
        gate = sb("gate", [P, 2, HIDDEN])
        hid = sb("hid", [P, 2, HIDDEN])
        hid_t = sb("hid_t", [P, 2, 2, P])
        y_sb = sb("y_sb", [P, XB, DIM])

        res = sb("res", [P, 2, TPB, 2, DIM])

        ps = ctx.enter_context(nc.psum_tensor("ps", [P, 8, 512], F32))

        names = """waited x2_free consts w_loaded x_loaded x_used ln1_var r12_ready ln1_coef yn_ready s_ready xT_mm xT_ev q_mm k_mm
            q_read k_read q_ready k_ready values_mm0 values_mm1 values_ev0 values_ev1 sc_mm sc_max sc_sub sc_exp sc_tr
            vo_mm ao_mm x2_ready ln2_var ln2_coef x3_ready x3T_mm x3T_ev lg_mm lg_sub
            lg_exp chosen_ready pos_mm slots_ready x2_stored0 x2_stored1 scattered
            row_2_ready pool_chain tables padded zeroed halo
            g_mm g_silu h_ready hT_mm hT_ev y_mm y_ev
            gT_mm gT_ev res_loaded0 res_loaded1
            summed out_stored  pads_ready""".split()
        S = {n: sem(n) for n in names}
        x2_stored = [S["x2_stored0"], S["x2_stored1"]]
        values_mm = [S["values_mm0"], S["values_mm1"]]
        values_ev = [S["values_ev0"], S["values_ev1"]]
        xg_loaded = [sem(f"xg_loaded{n}") for n in range(XB)]
        y_stored = [sem(f"y_stored{n}") for n in range(XB)]
        res_loaded = [S["res_loaded0"], S["res_loaded1"]]

        def wait_apart(eng, semaphore, value):
            eng.wait_ge(semaphore, value)
            eng.sem_inc(S["waited"], 1)

        class Chain:
            def __init__(self, eng, name, length):
                self.eng, self.n = eng, length
                self.sems = [sem(f"{name}{k}") for k in range(length)]

            def turn(self, count):
                assert self.n == len(self.sems), (self.n, len(self.sems))
                self.count, self.n = count, 0

            def did(self, ins):
                ins.then_inc(self.sems[self.n], 1)

            def due(self, apart=False):
                (wait_apart if apart else type(self.eng).wait_ge)(self.eng, self.sems[self.n], self.count)
                self.n += 1

            def link(self, ins, apart=False):
                self.did(ins)
                self.due(apart)

        def kept(eng, count):
            return count if isinstance(count, int) else eng.snap(count)

        def read_table(eng, table, start, count, largest):
            _, values = nc.values_load_multi_w_load_instructions(
                table[0:1, bass.ds(start, count)], engines=[eng.engine], min_val=0, max_val=largest,
                skip_runtime_bounds_check_because="the table's entries are clamped when it is made")
            return values

        def run_halves(eng, front, step):
            def two(i, first, last):
                c1, c2 = kept(eng, i + 1), kept(eng, i + 2)
                step(i, 0, None if first else kept(eng, i), c1, c2)
                step(i + 1, 1, c1, c2, None if last else kept(eng, i + 3))

            front(0, 0, 1)
            two(0, True, False)
            with eng.Fori(1, BATCH - 1) as c:
                two(c * 2, False, False)
            two(HALVES - 2, False, True)

        def last_pair(i):
            return isinstance(i, int) and i >= HALVES - 2

        x_h = x.rearrange("b (t p) d -> b p t d", p=P)
        res_h = results.rearrange("(b t p k) d -> b p t k d", t=TPB, p=P, k=2)
        out_h = out.rearrange("b (t p) d -> b p t d", p=P)
        block = ctx.enter_context(nc.Block())

        @block.sync
        def _(sp):
            sp.dma_start(x_t[:], x_h[0]).then_inc(S["x_loaded"], 16)
            for dst, src in ((ident, ident_in), (small, small_in), (rows, row_in), (lnw, ln_w), (lnb, ln_b),
                             (w_v, w_v_in), (w_qk, w_qk_t), (w_rot, w_rot_t), (w_o, w_out_t), (w_r, router_t),
                             (cos_sb, cos), (sin_sb, sin)):
                sp.dma_start(dst[:], src).then_inc(S["consts"], 16)
            sp.dma_start(squares[:], squares_in).then_inc(S["consts"], 16)
            sp.dma_start(w13_sb[:], w13.rearrange("e p n -> p e n")).then_inc(S["w_loaded"], 16)
            sp.dma_start(w2_sb[:], w2.rearrange("e (c p) n -> p e c n", p=P)).then_inc(S["w_loaded"], 16)

            def store_x2(i, h, n):
                sp.wait_ge(S["x2_ready"], n)
                sp.dma_start(x2_all[:, bass.ds(i * TPH, TPH), :], x2[:, h]).then_inc(x2_stored[h], 16)
                sp.wait_ge(x2_stored[h], i // 2 * 16 + 16)
                sp.sem_inc(S["x2_free"], 1)

            def step(i, h, n0, n, n1):
                if h == 0 and not last_pair(i):
                    sp.wait_ge(S["x_used"], (i // 2 + 1) * 2)
                    sp.dma_start(x_t[:], x_h[bass.ds(i // 2 + 1, 1)].rearrange("b p t d -> p (b t) d"))\
                        .then_inc(S["x_loaded"], 16)
                store_x2(i, h, n)

            run_halves(sp, lambda i, h, n: None, step)

            sp.wait_ge(S["tables"], 1)
            sp.wait_ge(S["pads_ready"], 3)
            sp.wait_ge(S["scattered"], HALVES * 2 * TPH * 16)
            for e in range(E):
                at = sp.value_load(pad_at[0:1, e:e + 1], min_val=e * REGION, max_val=e * REGION + TOKENS)
                sp.dma_start(expert_rows[bass.ds(at, P), :], pad_rows[:]).then_inc(S["padded"], 16)
            sp.dma_start(expert_rows[E * REGION:E * REGION + P, :], pad_rows[:]).then_inc(S["padded"], 16)
            sp.wait_ge(S["padded"], 16 * (E + 1))

            def load_rows(at, n):
                sp.dma_start(xg[:, n, :], expert_rows[bass.ds(at, P), :]).then_inc(xg_loaded[n], 16)

            for n, at in enumerate(read_table(sp, tile_row, 0, XB, E * REGION)):
                load_rows(at, n)
            with sp.Fori(1, MOE_TILES // XB) as m:
                for n, at in enumerate(read_table(sp, tile_row, m * XB, XB, E * REGION)):
                    sp.wait_ge(y_stored[n], m * 16)
                    load_rows(at, n)
            full = MOE_TILES // XB
            for n, at in enumerate(read_table(sp, tile_row, full * XB, MOE_TILES - full * XB, E * REGION)):
                sp.wait_ge(y_stored[n], full * 16)
                load_rows(at, n)

            for n in range(XB):
                sp.wait_ge(y_stored[n], 16 * len(range(n, MOE_TILES, XB)))
            for b in range(BATCH):
                if b >= 2:
                    sp.wait_ge(S["summed"], b - 1)
                sp.dma_start(res[:, b % 2], res_h[b]).then_inc(res_loaded[b % 2], 16)
                if b >= 1:
                    sp.wait_ge(S["summed"], b)
                    sp.dma_start(out_h[b - 1], x2_all[:, (b - 1) * TPB:b * TPB, :]).then_inc(S["out_stored"], 16)
            sp.wait_ge(S["summed"], BATCH)
            sp.dma_start(out_h[BATCH - 1], x2_all[:, (BATCH - 1) * TPB:, :]).then_inc(S["out_stored"], 16)
            sp.wait_ge(S["out_stored"], 16 * BATCH)

        @block.gpsimd
        def _(pool):
            pool.memset(minus_half[:], -0.5).then_inc(S["pool_chain"], 1)
            pool.memset(prob_t[:], 0.0).then_inc(S["zeroed"], 1)
            pool.memset(run[:], 0.0).then_inc(S["zeroed"], 1)
            for k in range(2):
                for h in range(2):
                    pool.iota(rowbuf[:, h, k, :, DIM:DIM + 1].bitcast(I32), pattern=[[2 * P, TPH], [0, 1]],
                              base=2 * (h * HALF) + k - 2 * SEQ, channel_multiplier=2).then_inc(S["pool_chain"], 1)
            pool.wait_ge(S["pool_chain"], 5)
            pool.memset(pad_rows[:, 0:DIM], 0.0).then_inc(S["pads_ready"], 1)
            pool.memset(pad_rows[:, DIM + 1:ROW], 0.0).then_inc(S["pads_ready"], 1)
            pool.iota(pad_rows[:, DIM:DIM + 1].bitcast(I32), pattern=[[0, 1]], base=NOWHERE,
                      channel_multiplier=0).then_inc(S["pads_ready"], 1)

            ln1 = Chain(pool, "roots1_link", 5)
            ln2 = Chain(pool, "roots2_link", 1)
            rt = Chain(pool, "dispatch_link", 2)

            def roots1(n_b):
                ln1.turn(n_b)
                var, mean = mv1[:, :, 1], mv1[:, :, 0]
                wait_apart(pool, S["ln1_var"], n_b)
                ln1.did(pool.tensor_scalar(var12, var, 1.0 + EPS, EPS * EPS, ALU.mult, ALU.add))
                ln1.due(apart=True)
                pool.tensor_tensor(r12, var12, minus_half[:], ALU.pow).then_inc(S["r12_ready"], 1)
                ln1.link(pool.tensor_scalar(var1, var, EPS, None, ALU.add), apart=True)
                ln1.link(pool.tensor_tensor(r1, var1, minus_half[:], ALU.pow), apart=True)
                ln1.link(pool.tensor_tensor(m_r1, mean, r1, ALU.mult), apart=True)
                ln1.link(pool.tensor_scalar(s_scale, r1, 1.0, None, ALU.add), apart=True)
                pool.tensor_scalar(s_bias, m_r1, -1.0, None, ALU.mult).then_inc(S["ln1_coef"], 1)

            def step(i, h, n0, n, n1):
                if h == 0 and not last_pair(i):
                    roots1(kept(pool, i // 2 + 2))
                ln2.turn(n)
                wait_apart(pool, S["ln2_var"], n)
                ln2.link(pool.tensor_scalar(ve2[:], mv2[:, :, 1], EPS, None, ALU.add), apart=True)
                pool.tensor_tensor(r2[:], ve2[:], minus_half[:, 0:TPH], ALU.pow).then_inc(S["ln2_coef"], 1)
                if n0 is not None:
                    dispatch(1 - h, n0)
                rt.turn(n)
                place = rowbuf[:, h, :, :, DIM:DIM + 1].bitcast(I32).rearrange("p k t o -> p (k t) o")
                rt.link(pool.tensor_scalar(place, place, 2.0 * SEQ, None, ALU.add), apart=True)
                wait_apart(pool, S["x3_ready"], n)
                rt.link(pool.tensor_copy(rowbuf[:, h, 1, :, 0:DIM], rowbuf[:, h, 0, :, 0:DIM]), apart=True)
                if n0 is not None:
                    wait_apart(pool, S["scattered"], 2 * TPH * 16 * i)

            def dispatch(h, n):
                wait_apart(pool, S["slots_ready"], n)
                for k in range(2):
                    for t in range(TPH):
                        pool.indirect_dma_start(
                            expert_rows[:, :], bass.IndirectOffsetOnAxis(ap=slots[:, h, k, t:t + 1], axis=0),
                            rowbuf[:, h, k, t, :], None).then_inc(S["scattered"], 16)

            roots1(1)
            run_halves(pool, lambda i, h, n: None, step)
            dispatch(1, HALVES)

            def store(n):
                pool.indirect_dma_start(
                    results[:, :], bass.IndirectOffsetOnAxis(ap=xg[:, n, DIM:DIM + 1].bitcast(I32), axis=0),
                    y_sb[:, n, :], None, bounds_check=2 * TOKENS - 1, oob_is_err=False).then_inc(y_stored[n], 16)

            with pool.Fori(0, MOE_TILES // XB) as m:
                for n in range(XB):
                    wait_apart(pool, S["y_ev"], m * XB + n + 1)
                    store(n)
            for j in range(MOE_TILES // XB * XB, MOE_TILES):
                pool.wait_ge(S["y_ev"], j + 1)
                store(j % XB)

        @block.tensor
        def _(pe):
            mm, tr = pe.matmul, pe.transpose

            def transpose_x(h, n):
                pe.wait_ge(S["yn_ready"], n)
                for t in range(TPH):
                    last = tr(ps[:, 0, t * P:(t + 1) * P], y_n[:, h * TPH + t, :], ident[:])
                last.then_inc(S["xT_mm"], 1)

            def project(h, c, done):
                xt = xn_t[:, BLOCK + h * HALF:BLOCK + (h + 1) * HALF]
                mm(ps[:, 2 + 2 * c, :], w_qk[:, c * DIM:(c + 1) * DIM], xt, start=True, stop=True)
                mm(ps[:, 3 + 2 * c, :], w_rot[:, c * DIM:(c + 1) * DIM], xt, start=True, stop=True).then_inc(done, 1)

            def project_v(h, s, n):
                pe.wait_ge(S["k_read" if s else "q_read"], n)
                for t in range(TPH):
                    at = (BLOCK if s == 0 else 0) + h * HALF + t * P
                    last = mm(ps[:, 2 + 2 * s + t // 2, t % 2 * 2 * DIM:(t % 2 + 1) * 2 * DIM],
                              xn_t[:, at:at + P], w_vo[:].rearrange("p a d -> p (a d)"), start=True, stop=True)
                last.then_inc(values_mm[s], 1)

            def scores(i, h, n):
                pe.wait_ge(S["q_ready"], n)
                pe.wait_ge(S["k_ready"], n)
                for a in range(HEADS):
                    first = 1 if h == 0 else 0
                    if first:
                        mm(ps[:, a, 0:64], ident_bf, mask_bf[:, 0, :], start=True, stop=True)
                    mm(ps[:, a, 64 * first:64 * TPH], ident_bf,
                       mask_bf[:, 1:2, :].to_broadcast([P, TPH - first, 64]), start=not first, stop=True,
                       skip_group_check=True)
                for t in range(TPH):
                    for g in range(P // BLOCK):
                        at = h * HALF + t * P + g * BLOCK
                        for a in range(HEADS):
                            last = mm(ps[g * BLOCK:(g + 1) * BLOCK, a, t * 64:(t + 1) * 64],
                                      q_t[a * HEAD:(a + 1) * HEAD, at:at + BLOCK],
                                      k_t[a * HEAD:(a + 1) * HEAD, at:at + 2 * BLOCK],
                                      start=False, stop=True, skip_group_check=True)
                last.then_inc(S["sc_mm"], 1)

            def values(i, h, n):
                pe.wait_ge(S["sc_tr"], n)
                for t in range(TPH):
                    for a in range(HEADS):
                        for s in range(2):
                            last = mm(ps[:, 1, t * P:(t + 1) * P], prob_t[:, a * TPH + t, 1 - s, :],
                                      vo[:, s, t, a, :], start=(a == 0 and s == 0), stop=(a == 1 and s == 1))
                last.then_inc(S["ao_mm"], 1)

            def transpose_x3(h, n):
                pe.wait_ge(S["x3_ready"], n)
                for t in range(TPH):
                    last = tr(ps[:, 6, t * P:(t + 1) * P], rowbuf[:, h, 0, t, 0:DIM], ident[:])
                last.then_inc(S["x3T_mm"], 1)

            def logits(n):
                pe.wait_ge(S["x3T_ev"], n)
                for t in range(TPH):
                    last = mm(ps[:, 7, t * E:(t + 1) * E], x3_t[:, t * P:(t + 1) * P], w_r[:], start=True, stop=True)
                last.then_inc(S["lg_mm"], 1)

            def positions(n):
                pe.wait_ge(S["chosen_ready"], n)
                mm(ps[:, 7, 64:64 + TPH * E], before_bf, chosen[:].rearrange("p t e -> p (t e)"),
                   start=True, stop=True, skip_group_check=True)
                for t in range(TPH - 1):
                    later = TPH - 1 - t
                    mm(ps[:, 7, 64 + (t + 1) * E:64 + TPH * E], ones_bf,
                       chosen[:, t:t + 1, :].to_broadcast([P, later, E]), start=False, stop=True,
                       skip_group_check=True)
                for t in range(TPH):
                    last = mm(ps[:, 7, 64 + TPH * E:64 + (TPH + 1) * E], ones_bf, chosen[:, t, :],
                              start=False, stop=True, skip_group_check=True)
                last.then_inc(S["pos_mm"], 1)

            def front(i, h, n):
                transpose_x(h, n)
                pe.wait_ge(S["xT_ev"], n)
                project(h, 0, S["q_mm"])
                project(h, 1, S["k_mm"])
                project_v(h, 0, n)
                scores(i, h, n)
                project_v(h, 1, n)

            def step(i, h, n0, n, n1):
                if n1 is not None:
                    transpose_x(1 - h, n1)
                pe.wait_ge(values_ev[1], n)
                values(i, h, n)
                if n1 is not None:
                    pe.wait_ge(S["xT_ev"], n1)
                    project(1 - h, 0, S["q_mm"])
                    project(1 - h, 1, S["k_mm"])
                if n0 is not None:
                    positions(n0)
                if n1 is not None:
                    project_v(1 - h, 0, n1)
                    scores(i + 1, 1 - h, n1)
                transpose_x3(h, n)
                logits(n)
                if n1 is not None:
                    project_v(1 - h, 1, n1)

            pe.wait_ge(S["consts"], CONSTS)
            for a in range(HEADS):
                d = slice(a * HEAD, (a + 1) * HEAD)
                last = mm(ps[:, 4 + a, 0:DIM], w_v[d, :], w_o[d, :], start=True, stop=True)
            last.then_inc(S["vo_mm"], 1)
            pe.wait_ge(S["halo"], 4)
            pe.wait_ge(S["zeroed"], 2)
            run_halves(pe, front, step)
            positions(HALVES)

            def rows_t(j, n, p):
                pe.wait_ge(xg_loaded[n], (j // XB + 1) * 16)
                tr(ps[:, 2 + p, 0:P], xg[:, n, 0:DIM], ident[:]).then_inc(S["gT_mm"], 1)

            def hidden(j, p, e):
                pe.wait_ge(S["gT_ev"], j + 1)
                mm(ps[:, p, :], xg_t[:, p, :], w13_sb[:, bass.ds(e, 1), :], start=True, stop=True)\
                    .then_inc(S["g_mm"], 1)

            def hidden_t(j, p):
                pe.wait_ge(S["h_ready"], j + 1)
                for c in range(2):
                    last = tr(ps[:, 4 + p, c * P:(c + 1) * P], hid[:, p, c * P:(c + 1) * P], ident[:])
                last.then_inc(S["hT_mm"], 1)

            def result(j, p, e):
                pe.wait_ge(S["hT_ev"], j + 1)
                for c in range(2):
                    last = mm(ps[:, 6 + p, 0:DIM], hid_t[:, p, c, :], w2_sb[:, bass.ds(e, 1), c, :],
                              start=(c == 0), stop=(c == 1))
                last.then_inc(S["y_mm"], 1)

            pe.wait_ge(S["w_loaded"], 32)
            pe.wait_ge(S["tables"], 1)
            first = 2 + XB
            e = read_table(pe, tile_exp, 0, first, E - 1)
            rows_t(0, 0, 0)
            rows_t(1, 1, 1)
            hidden(0, 0, e[0])
            rows_t(2, 2, 0)
            hidden(1, 1, e[1])
            hidden_t(0, 0)

            def tile_turn(j, n, p, loaded, e, e_result):
                if loaded is not None:
                    pe.wait_ge(xg_loaded[n], loaded * 16)
                    tr(ps[:, 3 - p, 0:P], xg[:, n, 0:DIM], ident[:]).then_inc(S["gT_mm"], 1)
                hidden(j, p, e)
                hidden_t(j - 1, 1 - p)
                result(j - 2, p, e_result)

            for j in range(2, first):
                tile_turn(j, (j + 1) % XB, j % 2, (j + 1) // XB + 1, e[j], e[j - 2])
            full = (MOE_TILES - first) // XB
            with pe.Fori(0, full) as m:
                e = read_table(pe, tile_exp, m * XB + first - 2, XB + 2, E - 1)
                for n in range(XB):
                    tile_turn(m * XB + first + n, (first + n + 1) % XB, n % 2, m + (first + n + 1) // XB + 1,
                              e[n + 2], e[n])
            rest = first + full * XB
            e = read_table(pe, tile_exp, rest - 2, MOE_TILES - rest + 2, E - 1)
            for j in range(rest, MOE_TILES):
                tile_turn(j, (j + 1) % XB, j % 2, (j + 1) // XB + 1 if j + 1 < MOE_TILES else None,
                          e[j - rest + 2], e[j - rest])
            j = MOE_TILES
            hidden_t(j - 1, (j - 1) % 2)
            result(j - 2, j % 2, e[j - rest])
            result(j - 1, (j - 1) % 2, e[j - rest + 1])

        @block.scalar
        def _(act):
            ac = act.activation

            def front_x(i, h, n):
                act.wait_ge(S["xT_mm"], n)
                ac(xn_t[:, BLOCK + h * HALF:BLOCK + (h + 1) * HALF], ps[:, 0, :], ACT.Identity,
                   bias=lnb[:, 0:1], scale=lnw[:, 0:1]).then_inc(S["xT_ev"], 1)

            def take_values(s, n):
                act.wait_ge(values_mm[s], n)
                ac(vo[:, s].rearrange("p t a d -> p (t a d)"), ps[:, 2 + 2 * s:4 + 2 * s, :].rearrange("p b n -> p (b n)"),
                   ACT.Copy).then_inc(values_ev[s], 1)

            def x3_ev(n):
                act.wait_ge(S["x3T_mm"], n)
                ac(x3_t[:], ps[:, 6, :], ACT.Copy).then_inc(S["x3T_ev"], 1)

            def residual(i, h):
                act.wait_ge(S["ln1_coef"], kept(act, i // 2 + 1))
                for t in range(h * TPH, (h + 1) * TPH):
                    last = ac(s_t[:, t, :], x_t[:, t, :], ACT.Identity, bias=s_bias[:, t:t + 1],
                              scale=s_scale[:, t:t + 1])
                last.then_inc(S["s_ready"], 1)
                if h == 1:
                    act.wait_ge(S["s_ready"], i + 1)
                    act.sem_inc(S["x_used"], 1)

            def router_exp(n):
                act.wait_ge(S["lg_sub"], n)
                ac(ex[:], lg[:], ACT.Exp).then_inc(S["lg_exp"], 1)

            def front(i, h, n):
                front_x(i, h, n)
                residual(i, 0)
                residual(i + 1, 1)
                take_values(0, n)

            def step(i, h, n0, n, n1):
                act.wait_ge(S["sc_sub"], n)
                ac(prob[:], prob[:], ACT.Exp, scale=float(HEAD) ** -0.5).then_inc(S["sc_exp"], 1)
                take_values(1, n)
                if n1 is not None:
                    front_x(i + 1, 1 - h, n1)
                if n0 is not None:
                    router_exp(n0)
                if h == 1 and n1 is not None:
                    residual(i + 1, 0)
                    act.wait_ge(S["x2_ready"], n)
                    residual(i + 2, 1)
                if n1 is not None:
                    take_values(0, n1)
                x3_ev(n)

            act.wait_ge(S["consts"], CONSTS)
            ac(squares_bf[:].rearrange("p a c -> p (a c)"), squares[:], ACT.Copy).then_inc(S["halo"], 1)
            act.wait_ge(S["vo_mm"], 1)
            ac(w_vo[:], ps[:, 4:6, 0:DIM], ACT.Copy).then_inc(S["halo"], 1)
            run_halves(act, front, step)
            router_exp(HALVES)

            def silu(j, p):
                act.wait_ge(S["g_mm"], j + 1)
                ac(gate[:, p, :], ps[:, p, 0:HIDDEN], ACT.Silu).then_inc(S["g_silu"], 1)

            def rows_ev(j, p):
                act.wait_ge(S["gT_mm"], j + 1)
                ac(xg_t[:, p, :], ps[:, 2 + p, 0:P], ACT.Copy).then_inc(S["gT_ev"], 1)

            rows_ev(0, 0)
            rows_ev(1, 1)
            silu(0, 0)
            with act.Fori(0, (MOE_TILES - 3) // 2) as m:
                for n in range(2):
                    j = m * 2 + 2 + n
                    rows_ev(j, n)
                    silu(j - 1, 1 - n)
            for j in range(2 + (MOE_TILES - 3) // 2 * 2, MOE_TILES):
                rows_ev(j, j % 2)
                silu(j - 1, (j - 1) % 2)
            silu(MOE_TILES - 1, (MOE_TILES - 1) % 2)

        @block.vector
        def _(dve):
            tt, ts, red = dve.tensor_tensor, dve.tensor_scalar, dve.tensor_reduce
            ln1 = Chain(dve, "stats_link", 1)
            ln2 = Chain(dve, "ln2_link", 1)
            first_pick = Chain(dve, "first_pick_link", 7)
            second_pick = Chain(dve, "second_pick_link", 5)
            weigh = Chain(dve, "weight_link", 6)
            place = Chain(dve, "place_link", 6)
            sc = Chain(dve, "score_link", 4)

            def stats(n_b):
                ln1.turn(n_b)
                dve.wait_ge(S["x_loaded"], n_b * 16)
                for t in range(TPB):
                    last = dve.bn_stats(stat1[:, t, :], x_t[:, t, :])
                ln1.link(last, apart=True)
                for t in range(TPB):
                    last = dve.bn_aggr(mv1[:, t, :], stat1[:, t, :])
                last.then_inc(S["ln1_var"], 1)

            def norm(i, h, n):
                b1 = i // 2 + 1
                dve.wait_ge(S["r12_ready"], b1)
                for t in range(h * TPH, (h + 1) * TPH):
                    last = ts(y_n[:, t, :], x_t[:, t, :], mv1[:, t, 0:1], r12[:, t:t + 1], ALU.subtract, ALU.mult)
                last.then_inc(S["yn_ready"], 1)
                if h == 1:
                    dve.wait_ge(S["yn_ready"], n)
                    dve.sem_inc(S["x_used"], 1)

            def rotate_parts(h, n, c, made, read):
                at = slice(h * HALF, (h + 1) * HALF)
                dve.wait_ge(made, n)
                tt(rope[:, 2 * c, :], ps[:, 2 + 2 * c, :], cos_sb[:, at], ALU.mult)
                tt(rope[:, 2 * c + 1, :], ps[:, 3 + 2 * c, :], sin_sb[:, at], ALU.mult).then_inc(read, 1)

            def rotate_sum(h, n):
                dve.wait_ge(S["q_read"], n)
                tt(q_t[:, h * HALF:(h + 1) * HALF], rope[:, 0, :], rope[:, 1, :], ALU.add).then_inc(S["q_ready"], 1)
                dve.wait_ge(S["k_read"], n)
                tt(k_t[:, BLOCK + h * HALF:BLOCK + (h + 1) * HALF], rope[:, 2, :], rope[:, 3, :],
                   ALU.add).then_inc(S["k_ready"], 1)

            def softmax_a(i, h, n):
                sc.turn(n)
                s = ps[:, 0:2, 0:TPH * 64].rearrange("p a (t k) -> p a t k", k=64)
                dve.wait_ge(S["sc_mm"], n)
                sc.link(red(smax[:], s, AX.X, ALU.max))
                for a in range(HEADS):
                    last = tt(prob[:, a * TPH:(a + 1) * TPH, :],
                              ps[:, a, 0:TPH * 64].rearrange("p (t k) -> p t k", k=64),
                              smax[:, a * TPH:(a + 1) * TPH].unsqueeze(2).to_broadcast([P, TPH, 64]), ALU.subtract)
                last.then_inc(S["sc_sub"], 1)

            def softmax_b(i, h, n):
                dve.wait_ge(S["sc_exp"], n)
                sc.link(red(ssum[:], prob[:], AX.X, ALU.add))
                sc.link(dve.reciprocal(srec[:], ssum[:]))
                sc.link(tt(prob[:], prob[:], srec[:].unsqueeze(2).to_broadcast([P, HEADS * TPH, 64]), ALU.mult),
                        apart=True)
                for g in range(P // BLOCK):
                    q = slice(g * BLOCK, (g + 1) * BLOCK)
                    last = dve.transpose(prob_t[q, :, :, q].rearrange("p n s q -> p (n s) q"),
                                         prob[q].rearrange("p n (s k) -> p (n s) k", k=BLOCK))
                last.then_inc(S["sc_tr"], 1)

            def sum_x2(i, h, n):
                dve.wait_ge(S["s_ready"], n)
                dve.wait_ge(S["ao_mm"], n)
                dve.wait_ge(S["x2_free"], n)
                tt(x2[:, h].rearrange("p t d -> p (t d)"), ps[:, 1, :],
                   s_t[:, h * TPH:(h + 1) * TPH, :].rearrange("p t d -> p (t d)"), ALU.add)\
                    .then_inc(S["x2_ready"], 1)
                dve.wait_ge(S["x2_ready"], n)
                for t in range(TPH):
                    last = dve.bn_stats(stat2[:, t, :], x2[:, h, t, :])
                ln2.turn(n)
                ln2.link(last, apart=True)
                for t in range(TPH):
                    last = dve.bn_aggr(mv2[:, t, :], stat2[:, t, :])
                last.then_inc(S["ln2_var"], 1)

            def second_norm(i, h, n):
                dve.wait_ge(S["ln2_coef"], n)
                for t in range(TPH):
                    last = ts(rowbuf[:, h, 0, t, 0:DIM], x2[:, h, t, :], mv2[:, t, 0:1], r2[:, t:t + 1],
                              ALU.subtract, ALU.mult)
                last.then_inc(S["x3_ready"], 1)

            per_e = lambda a: a.unsqueeze(2).to_broadcast([P, TPH, E])
            rank = small[:, 0:E].unsqueeze(1).to_broadcast([P, TPH, E])
            top_p, second_p = t1[1], t1[3]
            first, second, masked = t8[2], t8[5], t8[6]
            total, total_eps, kept_sum, kept_rec = t1[5:9]
            row_of, row_1, row_2 = t8[0], t8[1], t8[3]

            def route_start(n):
                first_pick.turn(n)
                logit = ps[:, 7, 0:TPH * E].rearrange("p (t e) -> p t e", e=E)
                dve.wait_ge(S["lg_mm"], n)
                first_pick.link(red(t1[0][:], logit, AX.X, ALU.max))
                tt(lg[:], logit, per_e(t1[0][:]), ALU.subtract).then_inc(S["lg_sub"], 1)


            def route_first(n):
                same, key, top = t8[0], t8[1], t1[2]
                weigh.turn(n)
                dve.wait_ge(S["lg_exp"], n)
                first_pick.did(red(top_p[:], ex[:], AX.X, ALU.max))
                weigh.did(red(total[:], ex[:], AX.X, ALU.add))
                first_pick.due()
                first_pick.did(tt(same[:], ex[:], per_e(top_p[:]), ALU.is_equal))
                weigh.due()
                weigh.did(dve.scalar_tensor_tensor(out=total_eps[:], in0=total[:], scalar=1e-6, in1=top_p[:],
                                                   op0=ALU.mult, op1=ALU.add))
                first_pick.due()
                first_pick.link(tt(key[:], same[:], rank, ALU.mult))
                first_pick.link(red(top[:], key[:], AX.X, ALU.max))
                first_pick.link(tt(first[:], key[:], per_e(top[:]), ALU.is_equal))
                first_pick.link(dve.scalar_tensor_tensor(out=masked[:], in0=first[:], scalar=-4.0, in1=ex[:],
                                                         op0=ALU.mult, op1=ALU.add))

            def route_second(h, n):
                same, key, top = t8[3], t8[4], t1[4]
                second_pick.turn(n)
                second_pick.link(red(second_p[:], masked[:], AX.X, ALU.max))
                second_pick.did(tt(same[:], masked[:], per_e(second_p[:]), ALU.is_equal))
                weigh.due()
                weigh.did(tt(kept_sum[:], total_eps[:], second_p[:], ALU.add))
                second_pick.due()
                second_pick.did(tt(key[:], same[:], rank, ALU.mult))
                weigh.due()
                weigh.did(dve.reciprocal(kept_rec[:], kept_sum[:]))
                second_pick.due()
                second_pick.did(red(top[:], key[:], AX.X, ALU.max))
                weigh.due()
                weigh.did(tt(rowbuf[:, h, 0, :, DIM + 1], top_p[:], kept_rec[:], ALU.mult))
                second_pick.due()
                second_pick.did(tt(second[:], key[:], per_e(top[:]), ALU.is_equal))
                weigh.due()
                weigh.did(tt(rowbuf[:, h, 1, :, DIM + 1], second_p[:], kept_rec[:], ALU.mult))
                second_pick.due()
                tt(chosen[:], first[:], second[:], ALU.add).then_inc(S["chosen_ready"], 1)
                weigh.due()

            counts = ps[:, 7, 64:64 + (TPH + 1) * E].rearrange("p (t e) -> p t e", e=E)

            def places_1(n):
                place.turn(n)
                place.did(tt(base[:], run[:], small[:, E:2 * E], ALU.add))

            def places_2(n):
                dve.wait_ge(S["pos_mm"], n)
                place.due()
                place.did(tt(row_of[:], counts[:, 0:TPH, :], base[:].unsqueeze(1).to_broadcast([P, TPH, E]), ALU.add))

            def places_3(n):
                place.due()
                place.did(tt(row_1[:], row_of[:], first[:], ALU.mult))
                tt(row_2[:], row_of[:], second[:], ALU.mult).then_inc(S["row_2_ready"], 1)

            def places_4(n):
                place.due()
                place.did(red(slot_f[:, 0, :], row_1[:], AX.X, ALU.add))
                dve.wait_ge(S["row_2_ready"], n)
                place.due()
                place.did(red(slot_f[:, 1, :], row_2[:], AX.X, ALU.add))

            def places_5(h, n):
                place.due()
                place.did(tt(run[:], counts[:, TPH, :], run[:], ALU.add))
                dve.tensor_copy(slots[:, h], slot_f[:]).then_inc(S["slots_ready"], 1)
                place.due()

            def step(i, h, n0, n, n1):
                softmax_a(i, h, n)
                if n1 is not None:
                    norm(i + 1, 1 - h, n1)
                softmax_b(i, h, n)
                if n0 is not None:
                    route_start(n0)
                    route_first(n0)
                    route_second(1 - h, n0)
                if h == 0 and not last_pair(i):
                    stats(kept(dve, i // 2 + 2))
                sum_x2(i, h, n)
                if n1 is not None:
                    rotate_parts(1 - h, n1, 0, S["q_mm"], S["q_read"])
                    rotate_parts(1 - h, n1, 1, S["k_mm"], S["k_read"])
                    rotate_sum(1 - h, n1)
                if n0 is not None:
                    places_1(n0)
                    places_2(n0)
                    places_3(n0)
                    places_4(n0)
                    places_5(1 - h, n0)
                second_norm(i, h, n)

            def front(i, h, n):
                norm(i, h, n)
                rotate_parts(h, n, 0, S["q_mm"], S["q_read"])
                rotate_parts(h, n, 1, S["k_mm"], S["k_read"])
                rotate_sum(h, n)

            dve.sem_inc(S["x2_free"], 2)
            dve.memset(xn_t[:, 0:BLOCK], 0.0).then_inc(S["halo"], 1)
            dve.memset(k_t[:, 0:BLOCK], 0.0).then_inc(S["halo"], 1)
            stats(1)
            dve.wait_ge(S["consts"], CONSTS)
            dve.wait_ge(S["zeroed"], 2)
            run_halves(dve, front, step)
            route_start(HALVES)
            route_first(HALVES)
            route_second(1, HALVES)
            places_1(HALVES)
            places_2(HALVES)
            places_3(HALVES)
            places_4(HALVES)
            places_5(1, HALVES)

            ct = Chain(dve, "table_link", 13)
            ct.turn(1)
            lk = ct.link
            le = rows[0:1, 0:E * E].rearrange("o (e f) -> o e f", f=E)
            jj = rows[0:1, E * E:E * E + MOE_TILES * E].rearrange("o (j e) -> o j e", e=E)
            j128 = rows[0:1, E * E + MOE_TILES * E:]
            lk(tt(tb[0][:], run[0:1, :], small[0:1, E:2 * E], ALU.add))
            lk(dve.tensor_copy(pad_at[:], tb[0][:]))
            lk(ts(tb_i[:, 0, :], run[0:1, :], float(P - 1), None, ALU.add))
            lk(ts(tb_i[:, 1, :], tb_i[:, 0, :], 7, None, ALU.arith_shift_right))
            lk(dve.tensor_copy(tb[1][:], tb_i[:, 1, :]))
            lk(tt(tbe[:], le, tb[1][:].unsqueeze(1).to_broadcast([1, E, E]), ALU.mult))
            lk(red(tb[2][:], tbe[:], AX.X, ALU.add))
            lk(ts(tb[3][:], tb[1][:], -float(P), float(REGION), ALU.mult, ALU.add))
            lk(tt(tbj[0][:], tb[2][:].unsqueeze(1).to_broadcast([1, MOE_TILES, E]), jj, ALU.is_le))
            lk(tt(tbj[1][:], tbj[0][:], tb[3][:].unsqueeze(1).to_broadcast([1, MOE_TILES, E]), ALU.mult))
            lk(red(tj[0][:], tbj[1][:], AX.X, ALU.add))
            lk(tt(tj[1][:], tj[0][:], j128, ALU.add))
            dve.tensor_scalar(tile_row[:], tj[1][:], float(E * REGION), None, ALU.min)
            lk(red(tj[2][:], tbj[0][:], AX.X, ALU.add))
            dve.tensor_scalar(tile_exp[:], tj[2][:], float(E - 1), None, ALU.min).then_inc(S["tables"], 1)

            def gated(j, p):
                dve.wait_ge(S["g_silu"], j + 1)
                tt(hid[:, p, :], ps[:, p, HIDDEN:2 * HIDDEN], gate[:, p, :], ALU.mult).then_inc(S["h_ready"], 1)

            def hidden_ev(j, p):
                dve.wait_ge(S["hT_mm"], j + 1)
                dve.tensor_copy(hid_t[:, p].rearrange("p c q -> p (c q)"), ps[:, 4 + p, 0:2 * P])\
                    .then_inc(S["hT_ev"], 1)

            def result_ev(j, p, n, turn):
                dve.wait_ge(S["y_mm"], j + 1)
                if not isinstance(j, int) or j >= XB:
                    dve.wait_ge(y_stored[n], turn * 16)
                ts(y_sb[:, n, :], ps[:, 6 + p, 0:DIM], xg[:, n, DIM + 1:ROW], None, ALU.mult).then_inc(S["y_ev"], 1)

            def turn(j):
                gated(j, j % 2)
                if j >= 1:
                    hidden_ev(j - 1, (j - 1) % 2)
                if j >= 2:
                    result_ev(j - 2, j % 2, (j - 2) % XB, (j - 2) // XB)

            first = 2 + XB
            for j in range(first):
                turn(j)
            full = (MOE_TILES - first) // XB
            with dve.Fori(0, full) as m:
                for n in range(XB):
                    j = m * XB + first + n
                    gated(j, n % 2)
                    hidden_ev(j - 1, 1 - n % 2)
                    result_ev(j - 2, n % 2, n, m + 1)
            for j in range(first + full * XB, MOE_TILES):
                turn(j)
            j = MOE_TILES
            hidden_ev(j - 1, (j - 1) % 2)
            result_ev(j - 2, j % 2, (j - 2) % XB, (j - 2) // XB)
            result_ev(j - 1, (j - 1) % 2, (j - 1) % XB, (j - 1) // XB)

            dve.wait_ge(x2_stored[0], 16 * (HALVES // 2))
            dve.wait_ge(x2_stored[1], 16 * (HALVES // 2))
            for b in range(BATCH):
                dve.wait_ge(res_loaded[b % 2], 16 * (b // 2 + 1))
                tile = x2_all[:, b * TPB:(b + 1) * TPB, :]
                tt(tile, tile, res[:, b % 2, :, 0, :], ALU.add).then_inc(S["pads_ready"], 1)
                dve.wait_ge(S["pads_ready"], 3 + b + 1)
                tt(tile, tile, res[:, b % 2, :, 1, :], ALU.add).then_inc(S["summed"], 1)


def _tables():
    inv = (1.0 / np.float32(10000.0) ** (np.arange(0, HEAD, 2, dtype=np.float32) / np.float32(HEAD))).astype(np.float32)
    angle = (np.arange(SEQ, dtype=np.float32)[None, :] * inv[:, None]).astype(np.float32)
    cos = np.tile(np.cos(angle), (4, 1)).astype(np.float32)
    sin = np.sin(angle).astype(np.float32)
    sin = np.tile(np.concatenate([-sin, sin]), (2, 1)).astype(np.float32)
    k, m = np.arange(P)[:, None], np.arange(P)[None, :]
    q, key = np.arange(P)[:, None], np.arange(64)[None, :] - BLOCK
    dist = q % BLOCK - key
    seen = (dist >= 0) & (dist < BLOCK)
    start = seen & ((q >= BLOCK) | (key >= 0))
    mask = np.concatenate([np.where(s, 0.0, MASKED) for s in (start, seen)], axis=1)
    squares = np.concatenate([k == m, k < m, np.ones((P, P)), mask], axis=1).astype(np.float32)
    e = np.arange(EXPERTS)
    small = np.tile(np.concatenate([EXPERTS - e, e * REGION]).astype(np.float32), (P, 1))
    j = np.arange(MOE_TILES)
    row = np.concatenate([(e[None, :] <= e[:, None]).ravel(), np.repeat(j, EXPERTS), j * P]).astype(np.float32)
    return {"cos": cos, "sin": sin, "ident": (k == m).astype(np.float32), "small": small,
            "row": row[None, :], "squares": squares}


def kernel(L0_attn_x, L0_attn_ln_w, L0_attn_ln_b, L0_attn_w_qkv, L0_attn_w_out, L0_ffn_router_w,
           L0_ffn_w13, L0_ffn_w2):
    import concourse.bacc as bacc
    from concourse.bass_utils import run_bass_kernel_spmd

    qkv_t = np.asarray(L0_attn_w_qkv).T
    swap = np.arange(2 * DIM).reshape(-1, 2, HEAD // 2)[:, ::-1].ravel()
    arrays = {
        "x": L0_attn_x, "ln_w": np.asarray(L0_attn_ln_w)[:, None], "ln_b": np.asarray(L0_attn_ln_b)[:, None],
        "w_qk_t": qkv_t[:, :2 * DIM], "w_rot_t": qkv_t[:, swap], "w_v": np.asarray(L0_attn_w_qkv)[2 * DIM:],
        "w_out_t": np.asarray(L0_attn_w_out).T,
        "router_t": np.asarray(L0_ffn_router_w).T, "w13": L0_ffn_w13, "w2": L0_ffn_w2, **_tables(),
    }
    arrays = {n: np.ascontiguousarray(a) for n, a in arrays.items()}
    nc = bacc.Bacc("TRN2", target_bir_lowering=False, num_devices=1)
    args = [nc.dram_tensor(f"in_{n}", a.shape, mybir.dt.from_np(a.dtype), kind="ExternalInput").ap()
            for n, a in arrays.items()]
    args.append(nc.dram_tensor("out", (BATCH, SEQ, DIM), mybir.dt.float32, kind="ExternalOutput").ap())
    program(nc, *args)
    r = run_bass_kernel_spmd(nc, [{f"in_{n}": a for n, a in arrays.items()}], core_ids=[0])
    return r.results[0]["out"]
```

```python
import numpy as np
import concourse.bass as bass
from concourse import mybir
from contextlib import ExitStack

BATCH, SEQ, DIM = 4, 1024, 128
HEADS, HEAD, BLOCK = 2, 64, 32
EXPERTS, HIDDEN = 8, 256
P = 128
HALF = 512
TPH = HALF // P
TPB = SEQ // P
HALVES = BATCH * SEQ // HALF
TOKENS = BATCH * SEQ
REGION = TOKENS + P
MOE_TILES = 2 * TOKENS // P + EXPERTS - 1
ROW = DIM + 2
NOWHERE = 4 * TOKENS
WEIGHTS, CONSTS = 8 * 16, 5 * 16
XB = 14
EARLY = XB
LATE = MOE_TILES - EARLY
EPS = 1e-5
MASKED = -1e30


def program(nc, x, ln_w, ln_b, w_qk_t, w_rot_t, w_v_in, w_out_t, router_t, w13, w2, cos, sin, ident_in,
            small_in, row_in, squares_in, out):
    F32, F32R, BF16, I32 = mybir.dt.float32, mybir.dt.float32r, mybir.dt.bfloat16, mybir.dt.int32
    ACT, ALU, AX = mybir.ActivationFunctionType, mybir.AluOpType, mybir.AxisListType
    E = EXPERTS

    expert_rows = nc.dram_tensor("expert_rows", [E * REGION + P, ROW], F32).ap()
    results = nc.dram_tensor("results", [2 * TOKENS, DIM], F32).ap()

    ctx = ExitStack()
    with ctx:
        def sb(name, shape, dt=F32):
            return ctx.enter_context(nc.sbuf_tensor(name, shape, dt))

        def sem(name):
            return ctx.enter_context(nc.semaphore(name))

        ident = sb("ident", [P, P])
        squares = sb("squares", [P, 4 * P])
        squares_bf = sb("squares_bf", [P, 4, P], BF16)
        ident_bf = squares_bf[:, 0, :]
        before_bf = squares_bf[:, 1, :]
        ones_bf = squares_bf[:, 2, :]
        mask_bf = squares_bf[:, 3, :].rearrange("p (a c) -> p a c", a=2)
        small = sb("small", [P, 2 * E])
        rows = sb("rows", [1, E * E + MOE_TILES * E + MOE_TILES])
        lnw = sb("lnw", [P, 1])
        lnb = sb("lnb", [P, 1])
        w_qk = sb("w_qk", [P, 2 * DIM])
        w_v = sb("w_v", [P, DIM])
        w_vo = sb("w_vo", [P, HEADS, DIM])
        w_rot = sb("w_rot", [P, 2 * DIM])
        w_o = sb("w_o", [P, DIM])
        w_r = sb("w_r", [P, E])
        w13_split = sb("w13_split", [P, E, 2, 2 * HIDDEN], F32R)
        w2_sb = sb("w2_sb", [P, E, 2, DIM])
        cos_sb = sb("cos_sb", [P, SEQ])
        sin_sb = sb("sin_sb", [P, SEQ])
        pad_rows = sb("pad_rows", [P, ROW])
        minus_half = sb("minus_half", [P, TPB])

        x_t = sb("x_t", [P, 2, TPH, DIM])
        stat1 = sb("stat1", [P, 2, TPH, 6])
        mv1 = sb("mv1", [P, 2, TPH, 2])
        co = sb("co", [P, 9, 2, TPH])
        r12, y_bias, s_scale, s_bias = (co[:, n] for n in (1, 3, 7, 8))
        y_n = sb("y_n", [P, TPH, DIM])
        s_t = sb("s_t", [P, 2, TPH, DIM])
        xn_t = sb("xn_t", [P, BLOCK + SEQ])
        q_t = sb("q_t", [P, SEQ])
        k_t = sb("k_t", [P, BLOCK + SEQ])
        rope = sb("rope", [P, 4, HALF])
        vo = sb("vo", [P, 2, TPH, HEADS, DIM])
        prob = sb("prob", [P, HEADS * TPH, 64])
        prob_t = sb("prob_t", [P, HEADS * TPH, 2, P])
        smax = sb("smax", [P, HEADS * TPH])
        ssum = sb("ssum", [P, HEADS * TPH])
        srec = sb("srec", [P, HEADS * TPH])
        x2 = sb("x2", [P, 2, TPH, DIM])
        x2_all = sb("x2_all", [P, TOKENS // P, DIM])
        stat2 = sb("stat2", [P, TPH, 6])
        mv2 = sb("mv2", [P, TPH, 2])
        ve2 = sb("ve2", [P, TPH])
        r2 = sb("r2", [P, TPH])
        x3_bias = sb("x3_bias", [P, TPH])
        rowbuf = sb("rowbuf", [P, 2, 2, TPH, ROW])
        x3_t = sb("x3_t", [P, HALF])
        slots = sb("slots", [P, 2, 2, TPH], I32)
        lg = sb("lg", [P, TPH, E])
        ex = sb("ex", [P, TPH, E])
        t8 = [sb(f"t8_{n}", [P, TPH, E]) for n in range(7)]
        t1 = [sb(f"t1_{n}", [P, TPH]) for n in range(9)]
        base = sb("base", [P, E])
        slot_f = sb("slot_f", [P, 2, TPH])
        chosen = sb("chosen", [P, TPH, E], BF16)
        run = sb("run", [P, E])

        tb = [sb(f"tb_{n}", [1, E]) for n in range(3)]
        tiles = sb("tiles", [1, E])
        tiles_to = sb("tiles_to", [1, E])
        jump = sb("jump", [1, E])
        taken = sb("taken", [1, E + 1])
        late_start = sb("late_start", [1, LATE])
        tb_i = sb("tb_i", [1, 2, E], I32)
        tbe = sb("tbe", [1, E, E])
        ended = sb("ended", [1, MOE_TILES, E])
        jumps = sb("jumps", [1, MOE_TILES, E])
        tj = [sb(f"tj_{n}", [1, MOE_TILES]) for n in range(3)]
        pad_at = sb("pad_at", [1, E], I32)
        tile_row = sb("tile_row", [1, MOE_TILES], I32)
        tile_exp = sb("tile_exp", [1, MOE_TILES], I32)
        xg = sb("xg", [P, XB, ROW])
        xg_t = sb("xg_t", [P, 2, 2, P], F32R)
        table_loaded = sb("table_loaded", [P, 1])
        gate = sb("gate", [P, 2, HIDDEN])
        hid = sb("hid", [P, 2, HIDDEN])
        hid_t = sb("hid_t", [P, 2, 2, P])
        y_sb = sb("y_sb", [P, XB, DIM])

        res = sb("res", [P, BATCH, TPB, 2, DIM])
        w13_sb = res[:].rearrange("p b t k d -> p (b t k d)")[:, 0:E * 2 * HIDDEN].rearrange("p (e n) -> p e n", e=E)

        ps = ctx.enter_context(nc.psum_tensor("ps", [P, 8, 512], F32))

        names = """waited x2_free weights consts w_loaded w13_loaded w_high w_split low_ready x_loaded0 x_loaded1 x_used
            ln1_var y_coef ln1_coef yn_ready s_ready xT_mm xT_ev q_mm k_mm q_read k_read q_ready
            k_ready values_mm0 values_mm1 values_ev0 values_ev1 sc_mm sc_sub sc_exp sc_tr vo_mm
            vo_ready ao_mm x2_ready ln2_var ln2_coef x3_ready x3_copied place_ready x3T_mm
            x3T_ev lg_mm lg_sub lg_exp chosen_ready pos_mm slots_ready counts_read x2_stored0
            x2_stored1 scattered row_2_ready pool_chain pads_known early_tables tables rows_out
            padded zeroed halo taken_zeroed squares_ready g_mm g_silu h_ready hT_mm hT_ev y_mm
            y_ev gT_mm gT_ev half_summed summed out_stored pads_ready""".split()
        S = {n: sem(n) for n in names}
        x2_stored = [S["x2_stored0"], S["x2_stored1"]]
        x_loaded = [S["x_loaded0"], S["x_loaded1"]]
        values_mm = [S["values_mm0"], S["values_mm1"]]
        values_ev = [S["values_ev0"], S["values_ev1"]]
        xg_loaded = [sem(f"xg_loaded{n}") for n in range(XB)]
        y_stored = [sem(f"y_stored{n}") for n in range(XB)]
        res_loaded = [sem(f"res_loaded{b}") for b in range(BATCH)]

        def wait_apart(eng, semaphore, value):
            eng.wait_ge(semaphore, value)
            eng.sem_inc(S["waited"], 1)

        class Chain:
            def __init__(self, eng, name, length):
                self.eng, self.n = eng, length
                self.sems = [sem(f"{name}{k}") for k in range(length)]

            def turn(self, count):
                assert self.n == len(self.sems), (self.n, len(self.sems))
                self.count, self.n = count, 0

            def did(self, ins):
                ins.then_inc(self.sems[self.n], 1)

            def due(self, apart=False):
                (wait_apart if apart else type(self.eng).wait_ge)(self.eng, self.sems[self.n], self.count)
                self.n += 1

            def link(self, ins, apart=False):
                self.did(ins)
                self.due(apart)

        class Once:
            def __init__(self, eng, name):
                self.eng, self.sem, self.count = eng, sem(name), 0

            def did(self, ins):
                self.count += 1
                ins.then_inc(self.sem, 1)

            def due(self):
                self.eng.wait_ge(self.sem, self.count)

            def link(self, ins):
                self.did(ins)
                self.due()

        def kept(eng, count):
            return count if isinstance(count, int) else eng.snap(count)

        def read_table(eng, table, start, count, largest):
            _, values = nc.values_load_multi_w_load_instructions(
                table[0:1, bass.ds(start, count)], engines=[eng.engine], min_val=0, max_val=largest,
                skip_runtime_bounds_check_because="the table's entries are clamped when it is made")
            return values

        def run_halves(eng, front, step):
            def two(i, first, last):
                c1, c2 = kept(eng, i + 1), kept(eng, i + 2)
                step(i, 0, None if first else kept(eng, i), c1, c2)
                step(i + 1, 1, c1, c2, None if last else kept(eng, i + 3))

            front(0, 1)
            two(0, True, False)
            with eng.Fori(1, BATCH - 1) as c:
                two(c * 2, False, False)
            two(HALVES - 2, False, True)

        def last_pair(i):
            return isinstance(i, int) and i >= HALVES - 2

        x_h = x.rearrange("b (h t p) d -> (b h) p t d", h=2, p=P)
        res_h = results.rearrange("(b t p k) d -> b p t k d", t=TPB, p=P, k=2)
        out_h = out.rearrange("b (t p) d -> b p t d", p=P)
        block = ctx.enter_context(nc.Block())

        @block.sync
        def _(sp):
            sp.dma_start(x_t[:, 0], x_h[0]).then_inc(x_loaded[0], 16)
            for dst, src in ((ident, ident_in), (w_v, w_v_in), (w_o, w_out_t), (lnw, ln_w), (lnb, ln_b),
                             (w_qk, w_qk_t), (w_rot, w_rot_t), (w_r, router_t)):
                sp.dma_start(dst[:], src).then_inc(S["weights"], 16)
            sp.dma_start(x_t[:, 1], x_h[1]).then_inc(x_loaded[1], 16)
            for dst, src in ((cos_sb, cos), (sin_sb, sin), (squares, squares_in), (small, small_in), (rows, row_in)):
                sp.dma_start(dst[:], src).then_inc(S["consts"], 16)
            sp.dma_start(w13_sb, w13.rearrange("e p n -> p e n")).then_inc(S["w13_loaded"], 16)
            sp.dma_start(w2_sb[:], w2.rearrange("e (c p) n -> p e c n", p=P)).then_inc(S["w_loaded"], 16)

            def store_x2(i, h, n):
                sp.wait_ge(S["x2_ready"], n)
                sp.dma_start(x2_all[:, bass.ds(i * TPH, TPH), :], x2[:, h]).then_inc(x2_stored[h], 16)

            def step(i, h, before, n, after):
                if not last_pair(i):
                    sp.wait_ge(S["x_used"], n)
                    sp.dma_start(x_t[:, h], x_h[bass.ds(i + 2, 1)].rearrange("b p t d -> p (b t) d"))\
                        .then_inc(x_loaded[h], 16)
                if before is not None:
                    sp.wait_ge(x2_stored[1 - h], (i // 2 + h) * 16)
                    sp.sem_inc(S["x2_free"], 1)
                if after is None:
                    load_early()
                store_x2(i, h, n)

            def load_rows(at, n):
                sp.dma_start(xg[:, n, :], expert_rows[bass.ds(at, P), :]).then_inc(xg_loaded[n], 16)

            def load_early():
                sp.wait_ge(S["early_tables"], 1)
                sp.wait_ge(S["rows_out"], HALVES - 2)
                for n, at in enumerate(read_table(sp, tile_row, 0, EARLY, E * REGION)):
                    load_rows(at, n)

            run_halves(sp, lambda h, n: None, step)
            sp.wait_ge(S["pads_known"], 1)
            sp.wait_ge(S["pads_ready"], 3)
            for at in read_table(sp, pad_at, 0, E, (E - 1) * REGION + TOKENS):
                sp.dma_start(expert_rows[bass.ds(at, P), :], pad_rows[:]).then_inc(S["padded"], 16)
            sp.dma_start(expert_rows[E * REGION:E * REGION + P, :], pad_rows[:]).then_inc(S["padded"], 16)
            sp.wait_ge(S["tables"], 1)
            sp.wait_ge(S["scattered"], HALVES * 2 * TPH * 16)
            sp.wait_ge(S["padded"], 16 * (E + 1))

            with sp.Fori(1, MOE_TILES // XB) as m:
                for n, at in enumerate(read_table(sp, tile_row, m * XB, XB, E * REGION)):
                    sp.wait_ge(y_stored[n], m * 16)
                    load_rows(at, n)
            full = MOE_TILES // XB
            for n, at in enumerate(read_table(sp, tile_row, full * XB, MOE_TILES - full * XB, E * REGION)):
                sp.wait_ge(y_stored[n], full * 16)
                load_rows(at, n)

            for n in range(XB):
                sp.wait_ge(y_stored[n], 16 * len(range(n, MOE_TILES, XB)))
            for b in range(BATCH):
                sp.dma_start(res[:, b], res_h[b]).then_inc(res_loaded[b], 16)
            for b in range(BATCH):
                for part in range(2):
                    sp.wait_ge(S["summed"], 2 * b + part + 1)
                    t = slice(part * TPH, (part + 1) * TPH)
                    sp.dma_start(out_h[b][:, t, :], x2_all[:, b * TPB + part * TPH:b * TPB + (part + 1) * TPH, :])\
                        .then_inc(S["out_stored"], 16)
            sp.wait_ge(S["out_stored"], 16 * 2 * BATCH)

        @block.gpsimd
        def _(pool):
            pool.memset(minus_half[:], -0.5).then_inc(S["pool_chain"], 1)
            pool.memset(prob_t[:], 0.0).then_inc(S["zeroed"], 1)
            pool.memset(run[:], 0.0).then_inc(S["zeroed"], 1)
            for k in range(2):
                for h in range(2):
                    pool.iota(rowbuf[:, h, k, :, DIM:DIM + 1].bitcast(I32), pattern=[[2 * P, TPH], [0, 1]],
                              base=2 * (h * HALF) + k - 2 * SEQ, channel_multiplier=2).then_inc(S["pool_chain"], 1)
            pool.wait_ge(S["pool_chain"], 5)
            pool.memset(pad_rows[:, 0:DIM], 0.0).then_inc(S["pads_ready"], 1)
            pool.memset(pad_rows[:, DIM + 1:ROW], 0.0).then_inc(S["pads_ready"], 1)
            pool.iota(pad_rows[:, DIM:DIM + 1].bitcast(I32), pattern=[[0, 1]], base=NOWHERE,
                      channel_multiplier=0).then_inc(S["pads_ready"], 1)

            ln1 = Chain(pool, "roots1_link", 7)
            ln2 = Chain(pool, "roots2_link", 3)

            def roots1(h, n):
                ln1.turn(n)
                var, mean = mv1[:, h, :, 1], mv1[:, h, :, 0]
                var12, r12, m_r12, y_bias, var1, r1, m_r1, s_scale, s_bias = (co[:, c, h] for c in range(9))
                power = minus_half[:, 0:TPH]
                wait_apart(pool, S["ln1_var"], n)
                ln1.link(pool.tensor_scalar(var12, var, 1.0 + EPS, EPS * EPS, ALU.mult, ALU.add), apart=True)
                ln1.link(pool.tensor_tensor(r12, var12, power, ALU.pow), apart=True)
                ln1.link(pool.tensor_tensor(m_r12, mean, r12, ALU.mult), apart=True)
                pool.tensor_scalar(y_bias, m_r12, -1.0, None, ALU.mult).then_inc(S["y_coef"], 1)
                ln1.link(pool.tensor_scalar(var1, var, EPS, None, ALU.add), apart=True)
                ln1.link(pool.tensor_tensor(r1, var1, power, ALU.pow), apart=True)
                ln1.link(pool.tensor_tensor(m_r1, mean, r1, ALU.mult), apart=True)
                ln1.link(pool.tensor_scalar(s_scale, r1, 1.0, None, ALU.add), apart=True)
                pool.tensor_scalar(s_bias, m_r1, -1.0, None, ALU.mult).then_inc(S["ln1_coef"], 1)

            def rotate_q(h, n):
                wait_apart(pool, S["q_read"], n)
                pool.tensor_tensor(q_t[:, h * HALF:(h + 1) * HALF], rope[:, 0, :], rope[:, 1, :],
                                   ALU.add).then_inc(S["q_ready"], 1)

            def step(i, h, before, n, after):
                if after is not None:
                    rotate_q(1 - h, after)
                if not last_pair(i):
                    roots1(h, kept(pool, i + 3))
                ln2.turn(n)
                wait_apart(pool, S["ln2_var"], n)
                ln2.link(pool.tensor_scalar(ve2[:], mv2[:, :, 1], EPS, None, ALU.add), apart=True)
                ln2.link(pool.tensor_tensor(r2[:], ve2[:], minus_half[:, 0:TPH], ALU.pow), apart=True)
                ln2.link(pool.tensor_tensor(ve2[:], mv2[:, :, 0], r2[:], ALU.mult), apart=True)
                pool.tensor_scalar(x3_bias[:], ve2[:], -1.0, None, ALU.mult).then_inc(S["ln2_coef"], 1)
                if before is not None:
                    dispatch(1 - h, before)
                place = rowbuf[:, h, :, :, DIM:DIM + 1].bitcast(I32).rearrange("p k t o -> p (k t) o")
                pool.tensor_scalar(place, place, 2.0 * SEQ, None, ALU.add).then_inc(S["place_ready"], 1)
                if before is not None:
                    wait_apart(pool, S["scattered"], 2 * TPH * 16 * i)
                    pool.sem_inc(S["rows_out"], 1)
                else:
                    split_low(1)

            def dispatch(h, n):
                wait_apart(pool, S["place_ready"], n)
                wait_apart(pool, S["x3_ready"], n)
                wait_apart(pool, S["x3_copied"], n)
                wait_apart(pool, S["slots_ready"], n)
                for k in range(2):
                    for t in range(TPH):
                        pool.indirect_dma_start(
                            expert_rows[:, :], bass.IndirectOffsetOnAxis(ap=slots[:, h, k, t:t + 1], axis=0),
                            rowbuf[:, h, k, t, :], None).then_inc(S["scattered"], 16)

            def split_low(half):
                experts = slice(half * E // 2, (half + 1) * E // 2)
                wait_apart(pool, S["w_high"], half + 1)
                pool.tensor_tensor(w13_split[:, experts, 1, :], w13_sb[:, experts],
                                   w13_split[:, experts, 0, :].bitcast(F32), ALU.subtract).then_inc(S["w_split"], 1)

            def front(h, n):
                rotate_q(h, n)
                split_low(0)

            roots1(0, 1)
            roots1(1, 2)
            run_halves(pool, front, step)
            dispatch(1, HALVES)

            def store(n):
                pool.indirect_dma_start(
                    results[:, :], bass.IndirectOffsetOnAxis(ap=xg[:, n, DIM:DIM + 1].bitcast(I32), axis=0),
                    y_sb[:, n, :], None, bounds_check=2 * TOKENS - 1, oob_is_err=False).then_inc(y_stored[n], 16)

            with pool.Fori(0, MOE_TILES // XB) as m:
                for n in range(XB):
                    wait_apart(pool, S["y_ev"], m * XB + n + 1)
                    store(n)
            for j in range(MOE_TILES // XB * XB, MOE_TILES):
                pool.wait_ge(S["y_ev"], j + 1)
                store(j % XB)

        @block.tensor
        def _(pe):
            mm, tr = pe.matmul, pe.transpose

            def keep_busy(count):
                for _ in range(count):
                    mm(ps[:, 5, :], ident_bf, squares_bf[:].rearrange("p a c -> p (a c)"), start=True, stop=True)

            def transpose_x(h, n):
                pe.wait_ge(S["yn_ready"], n)
                for t in range(TPH):
                    last = tr(ps[:, 0, t * P:(t + 1) * P], y_n[:, t, :], ident[:])
                last.then_inc(S["xT_mm"], 1)

            def project(h, c, done):
                xt = xn_t[:, BLOCK + h * HALF:BLOCK + (h + 1) * HALF]
                mm(ps[:, 2 + 2 * c, :], w_qk[:, c * DIM:(c + 1) * DIM], xt, start=True, stop=True)
                mm(ps[:, 3 + 2 * c, :], w_rot[:, c * DIM:(c + 1) * DIM], xt, start=True, stop=True).then_inc(done, 1)

            def project_v(h, s, n):
                pe.wait_ge(S["k_read" if s else "q_read"], n)
                for t in range(TPH):
                    at = (BLOCK if s == 0 else 0) + h * HALF + t * P
                    last = mm(ps[:, 2 + 2 * s + t // 2, t % 2 * 2 * DIM:(t % 2 + 1) * 2 * DIM],
                              xn_t[:, at:at + P], w_vo[:].rearrange("p a d -> p (a d)"), start=True, stop=True)
                last.then_inc(values_mm[s], 1)

            def scores(h, n):
                pe.wait_ge(S["q_ready"], n)
                pe.wait_ge(S["k_ready"], n)
                for a in range(HEADS):
                    first = 1 if h == 0 else 0
                    if first:
                        mm(ps[:, a, 0:64], ident_bf, mask_bf[:, 0, :], start=True, stop=True)
                    mm(ps[:, a, 64 * first:64 * TPH], ident_bf,
                       mask_bf[:, 1:2, :].to_broadcast([P, TPH - first, 64]), start=not first, stop=True,
                       skip_group_check=True)
                for t in range(TPH):
                    for g in range(P // BLOCK):
                        at = h * HALF + t * P + g * BLOCK
                        for a in range(HEADS):
                            last = mm(ps[g * BLOCK:(g + 1) * BLOCK, a, t * 64:(t + 1) * 64],
                                      q_t[a * HEAD:(a + 1) * HEAD, at:at + BLOCK],
                                      k_t[a * HEAD:(a + 1) * HEAD, at:at + 2 * BLOCK],
                                      start=False, stop=True, skip_group_check=True)
                last.then_inc(S["sc_mm"], 1)

            def values(n):
                pe.wait_ge(S["sc_tr"], n)
                for t in range(TPH):
                    for a in range(HEADS):
                        for s in range(2):
                            last = mm(ps[:, 6, t * P:(t + 1) * P], prob_t[:, a * TPH + t, 1 - s, :],
                                      vo[:, s, t, a, :], start=(a == 0 and s == 0), stop=(a == 1 and s == 1))
                last.then_inc(S["ao_mm"], 1)

            def transpose_x3(h, n):
                pe.wait_ge(S["x3_ready"], n)
                for t in range(TPH):
                    last = tr(ps[:, 6, t * P:(t + 1) * P], rowbuf[:, h, 0, t, 0:DIM], ident[:])
                last.then_inc(S["x3T_mm"], 1)

            def logits(n):
                pe.wait_ge(S["x3T_ev"], n)
                for t in range(TPH):
                    last = mm(ps[:, 7, t * E:(t + 1) * E], x3_t[:, t * P:(t + 1) * P], w_r[:], start=True, stop=True)
                last.then_inc(S["lg_mm"], 1)

            def positions(n):
                pe.wait_ge(S["chosen_ready"], n)
                mm(ps[:, 7, 64:64 + TPH * E], before_bf, chosen[:].rearrange("p t e -> p (t e)"),
                   start=True, stop=True, skip_group_check=True)
                for t in range(TPH - 1):
                    later = TPH - 1 - t
                    mm(ps[:, 7, 64 + (t + 1) * E:64 + TPH * E], ones_bf,
                       chosen[:, t:t + 1, :].to_broadcast([P, later, E]), start=False, stop=True,
                       skip_group_check=True)
                for t in range(TPH):
                    last = mm(ps[:, 7, 64 + TPH * E:64 + (TPH + 1) * E], ones_bf, chosen[:, t, :],
                              start=False, stop=True, skip_group_check=True)
                last.then_inc(S["pos_mm"], 1)

            def front(h, n):
                transpose_x(h, n)
                for a in range(HEADS):
                    d = slice(a * HEAD, (a + 1) * HEAD)
                    last = mm(ps[:, 6 + a, 0:DIM], w_v[d, :], w_o[d, :], start=True, stop=True)
                last.then_inc(S["vo_mm"], 1)
                pe.wait_ge(S["halo"], 2)
                pe.wait_ge(S["xT_ev"], n)
                project(h, 0, S["q_mm"])
                project(h, 1, S["k_mm"])
                pe.wait_ge(S["vo_ready"], 1)
                project_v(h, 0, n)
                pe.wait_ge(S["squares_ready"], 1)
                scores(h, n)
                project_v(h, 1, n)

            def step(i, h, before, n, after):
                if after is not None:
                    pe.wait_ge(S["sc_sub"], n)
                    transpose_x(1 - h, after)
                if before is not None:
                    transpose_x3(1 - h, before)
                if after is not None:
                    pe.wait_ge(values_ev[0], n)
                    pe.wait_ge(S["xT_ev"], after)
                    project(1 - h, 0, S["q_mm"])
                if before is not None:
                    logits(before)
                pe.wait_ge(values_ev[1], n)
                if after is not None:
                    project(1 - h, 1, S["k_mm"])
                values(n)
                if after is not None:
                    scores(1 - h, after)
                    project_v(1 - h, 0, after)
                if before is not None:
                    positions(before)
                if after is not None:
                    project_v(1 - h, 1, after)

            def rows_t(j, n, p):
                pe.wait_ge(xg_loaded[n], (j // XB + 1) * 16)
                tr(ps[:, 2 + p, 0:P], xg[:, n, 0:DIM], ident[:]).then_inc(S["gT_mm"], 1)

            def hidden(j, p, e):
                pe.wait_ge(S["low_ready"], j + 1)
                mm(ps[:, p, :], xg_t[:, p, 0, :], w13_split[:, bass.ds(e, 1), 1, :], start=True, stop=False)
                mm(ps[:, p, :], xg_t[:, p, 0, :], w13_split[:, bass.ds(e, 1), 0, :], start=False, stop=False)
                mm(ps[:, p, :], xg_t[:, p, 1, :], w13_split[:, bass.ds(e, 1), 0, :], start=False, stop=True)\
                    .then_inc(S["g_mm"], 1)

            def hidden_t(j, p):
                pe.wait_ge(S["h_ready"], j + 1)
                for c in range(2):
                    last = tr(ps[:, 4 + p, c * P:(c + 1) * P], hid[:, p, c * P:(c + 1) * P], ident[:])
                last.then_inc(S["hT_mm"], 1)

            def result(j, p, e):
                pe.wait_ge(S["hT_ev"], j + 1)
                for c in range(2):
                    last = mm(ps[:, 6 + p, 0:DIM], hid_t[:, p, c, :], w2_sb[:, bass.ds(e, 1), c, :],
                              start=(c == 0), stop=(c == 1))
                last.then_inc(S["y_mm"], 1)

            pe.wait_ge(S["weights"], WEIGHTS)
            run_halves(pe, front, step)

            pe.wait_ge(S["w_loaded"], 16)
            pe.wait_ge(S["w_split"], 2)
            pe.wait_ge(S["early_tables"], 1)
            e = list(read_table(pe, tile_exp, 0, EARLY, E - 1))
            keep_busy(4)
            rows_t(0, 0, 0)
            rows_t(1, 1, 1)
            hidden(0, 0, e[0])
            hidden(1, 1, e[1])

            pe.wait_ge(S["slots_ready"], HALVES - 1)
            transpose_x3(1, HALVES)
            keep_busy(2)
            logits(HALVES)
            rows_t(2, 2, 0)
            keep_busy(10)
            positions(HALVES)

            first = 2 + XB
            hidden_t(0, 0)

            def tile_turn(j, n, p, loaded, e, e_result):
                if loaded is not None:
                    pe.wait_ge(xg_loaded[n], loaded * 16)
                    tr(ps[:, 3 - p, 0:P], xg[:, n, 0:DIM], ident[:]).then_inc(S["gT_mm"], 1)
                hidden(j, p, e)
                hidden_t(j - 1, 1 - p)
                result(j - 2, p, e_result)

            for j in range(2, first):
                if j == EARLY:
                    pe.wait_ge(S["tables"], 1)
                    e += read_table(pe, tile_exp, EARLY, first - EARLY, E - 1)
                tile_turn(j, (j + 1) % XB, j % 2, (j + 1) // XB + 1, e[j], e[j - 2])
            full = (MOE_TILES - first) // XB
            with pe.Fori(0, full) as m:
                e = read_table(pe, tile_exp, m * XB + first - 2, XB + 2, E - 1)
                for n in range(XB):
                    tile_turn(m * XB + first + n, (first + n + 1) % XB, n % 2, m + (first + n + 1) // XB + 1,
                              e[n + 2], e[n])
            rest = first + full * XB
            e = read_table(pe, tile_exp, rest - 2, MOE_TILES - rest + 2, E - 1)
            for j in range(rest, MOE_TILES):
                tile_turn(j, (j + 1) % XB, j % 2, (j + 1) // XB + 1 if j + 1 < MOE_TILES else None,
                          e[j - rest + 2], e[j - rest])
            j = MOE_TILES
            hidden_t(j - 1, (j - 1) % 2)
            result(j - 2, j % 2, e[j - rest])
            result(j - 1, (j - 1) % 2, e[j - rest + 1])

        @block.scalar
        def _(act):
            ac = act.activation

            def silu(j, p):
                act.wait_ge(S["g_mm"], j + 1)
                ac(gate[:, p, :], ps[:, p, 0:HIDDEN], ACT.Silu).then_inc(S["g_silu"], 1)

            def rows_ev(j, p):
                act.wait_ge(S["gT_mm"], j + 1)
                ac(xg_t[:, p, 0, :], ps[:, 2 + p, 0:P], ACT.Copy).then_inc(S["gT_ev"], 1)

            def normalise(h, n):
                act.wait_ge(S["y_coef"], n)
                for t in range(TPH):
                    last = ac(y_n[:, t, :], x_t[:, h, t, :], ACT.Identity, bias=y_bias[:, h, t:t + 1],
                              scale=r12[:, h, t:t + 1])
                last.then_inc(S["yn_ready"], 1)

            def front_x(h, n):
                act.wait_ge(S["xT_mm"], n)
                ac(xn_t[:, BLOCK + h * HALF:BLOCK + (h + 1) * HALF], ps[:, 0, :], ACT.Identity,
                   bias=lnb[:, 0:1], scale=lnw[:, 0:1]).then_inc(S["xT_ev"], 1)

            def take_values(s, n):
                act.wait_ge(values_mm[s], n)
                ac(vo[:, s].rearrange("p t a d -> p (t a d)"),
                   ps[:, 2 + 2 * s:4 + 2 * s, :].rearrange("p b n -> p (b n)"), ACT.Copy).then_inc(values_ev[s], 1)

            def second_norm(h, n):
                act.wait_ge(S["ln2_coef"], n)
                for t in range(TPH):
                    last = ac(rowbuf[:, h, 0, t, 0:DIM], x2[:, h, t, :], ACT.Identity, bias=x3_bias[:, t:t + 1],
                              scale=r2[:, t:t + 1])
                last.then_inc(S["x3_ready"], 1)

            def x3_ev(n):
                act.wait_ge(S["x3T_mm"], n)
                ac(x3_t[:], ps[:, 6, :], ACT.Copy).then_inc(S["x3T_ev"], 1)

            def copy_x3(h, n):
                act.wait_ge(S["x3_ready"], n)
                ac(rowbuf[:, h, 1, :, 0:DIM], rowbuf[:, h, 0, :, 0:DIM], ACT.Copy).then_inc(S["x3_copied"], 1)

            def residual(h, n):
                act.wait_ge(S["ln1_coef"], n)
                for t in range(TPH):
                    last = ac(s_t[:, h, t, :], x_t[:, h, t, :], ACT.Identity, bias=s_bias[:, h, t:t + 1],
                              scale=s_scale[:, h, t:t + 1])
                last.then_inc(S["s_ready"], 1)
                act.wait_ge(S["yn_ready"], n)
                act.wait_ge(S["s_ready"], n)
                act.sem_inc(S["x_used"], 1)

            def router_exp(n):
                act.wait_ge(S["lg_sub"], n)
                ac(ex[:], lg[:], ACT.Exp).then_inc(S["lg_exp"], 1)

            def split_high(experts):
                act.wait_ge(S["w13_loaded"], 16)
                ac(w13_split[:, experts, 0, :], w13_sb[:, experts], ACT.Copy).then_inc(S["w_high"], 1)

            def front(h, n):
                normalise(h, n)
                act.wait_ge(S["weights"], WEIGHTS)
                front_x(h, n)
                act.wait_ge(S["vo_mm"], 1)
                ac(w_vo[:], ps[:, 6:8, 0:DIM], ACT.Copy).then_inc(S["vo_ready"], 1)
                act.wait_ge(S["consts"], CONSTS)
                ac(squares_bf[:].rearrange("p a c -> p (a c)"), squares[:], ACT.Copy).then_inc(S["squares_ready"], 1)
                residual(h, n)
                normalise(1, 2)
                take_values(0, n)
                split_high(slice(0, E // 2))

            def step(i, h, before, n, after):
                act.wait_ge(S["sc_sub"], n)
                ac(prob[:], prob[:], ACT.Exp, scale=float(HEAD) ** -0.5).then_inc(S["sc_exp"], 1)
                if after is not None:
                    front_x(1 - h, after)
                take_values(1, n)
                if before is not None:
                    x3_ev(before)
                    copy_x3(1 - h, before)
                if after is not None:
                    residual(1 - h, after)
                if before is not None:
                    router_exp(before)
                else:
                    split_high(slice(E // 2, E))
                if not last_pair(i):
                    normalise(h, kept(act, i + 3))
                if after is not None:
                    take_values(0, after)
                else:
                    rows_ev(0, 0)
                    rows_ev(1, 1)
                second_norm(h, n)

            run_halves(act, front, step)
            x3_ev(HALVES)
            copy_x3(1, HALVES)
            router_exp(HALVES)

            ac(table_loaded[:], lnw[:, 0:1], ACT.Silu)
            silu(0, 0)
            with act.Fori(0, (MOE_TILES - 3) // 2) as m:
                for n in range(2):
                    j = m * 2 + 2 + n
                    rows_ev(j, n)
                    silu(j - 1, 1 - n)
            for j in range(2 + (MOE_TILES - 3) // 2 * 2, MOE_TILES):
                rows_ev(j, j % 2)
                silu(j - 1, (j - 1) % 2)
            silu(MOE_TILES - 1, (MOE_TILES - 1) % 2)

        @block.vector
        def _(dve):
            tt, ts, red = dve.tensor_tensor, dve.tensor_scalar, dve.tensor_reduce
            ln1 = Chain(dve, "stats_link", 1)
            ln2 = Chain(dve, "ln2_link", 1)
            first_pick = Chain(dve, "first_pick_link", 7)
            second_pick = Chain(dve, "second_pick_link", 5)
            weigh = Chain(dve, "weight_link", 6)
            place = Chain(dve, "place_link", 5)
            sc = Chain(dve, "score_link", 4)

            def stats(h, turns, n):
                ln1.turn(n)
                dve.wait_ge(x_loaded[h], turns * 16)
                for t in range(TPH):
                    last = dve.bn_stats(stat1[:, h, t, :], x_t[:, h, t, :])
                ln1.link(last, apart=True)
                for t in range(TPH):
                    last = dve.bn_aggr(mv1[:, h, t, :], stat1[:, h, t, :])
                last.then_inc(S["ln1_var"], 1)

            def rotate_parts(h, n, c, made, read):
                at = slice(h * HALF, (h + 1) * HALF)
                dve.wait_ge(made, n)
                tt(rope[:, 2 * c, :], ps[:, 2 + 2 * c, :], cos_sb[:, at], ALU.mult)
                tt(rope[:, 2 * c + 1, :], ps[:, 3 + 2 * c, :], sin_sb[:, at], ALU.mult).then_inc(read, 1)

            def rotate_k(h, n):
                dve.wait_ge(S["k_read"], n)
                tt(k_t[:, BLOCK + h * HALF:BLOCK + (h + 1) * HALF], rope[:, 2, :], rope[:, 3, :],
                   ALU.add).then_inc(S["k_ready"], 1)

            def softmax_a(n):
                sc.turn(n)
                s = ps[:, 0:2, 0:TPH * 64].rearrange("p a (t k) -> p a t k", k=64)
                dve.wait_ge(S["sc_mm"], n)
                sc.link(red(smax[:], s, AX.X, ALU.max))
                tt(prob[:].rearrange("p (a t) k -> p a t k", a=HEADS), s,
                   smax[:].rearrange("p (a t) -> p a t", a=HEADS).unsqueeze(3).to_broadcast([P, HEADS, TPH, 64]),
                   ALU.subtract).then_inc(S["sc_sub"], 1)

            def softmax_b(n):
                dve.wait_ge(S["sc_exp"], n)
                sc.link(red(ssum[:], prob[:], AX.X, ALU.add))
                sc.link(dve.reciprocal(srec[:], ssum[:]))
                sc.link(tt(prob[:], prob[:], srec[:].unsqueeze(2).to_broadcast([P, HEADS * TPH, 64]), ALU.mult),
                        apart=True)
                for g in range(P // BLOCK):
                    q = slice(g * BLOCK, (g + 1) * BLOCK)
                    last = dve.transpose(prob_t[q, :, :, q].rearrange("p n s q -> p (n s) q"),
                                         prob[q].rearrange("p n (s k) -> p (n s) k", k=BLOCK))
                last.then_inc(S["sc_tr"], 1)

            def sum_x2(h, n):
                dve.wait_ge(S["s_ready"], n)
                dve.wait_ge(S["ao_mm"], n)
                dve.wait_ge(S["x2_free"], n)
                tt(x2[:, h].rearrange("p t d -> p (t d)"), ps[:, 6, :],
                   s_t[:, h].rearrange("p t d -> p (t d)"), ALU.add)\
                    .then_inc(S["x2_ready"], 1)
                dve.wait_ge(S["x2_ready"], n)
                for t in range(TPH):
                    last = dve.bn_stats(stat2[:, t, :], x2[:, h, t, :])
                ln2.turn(n)
                ln2.link(last, apart=True)
                for t in range(TPH):
                    last = dve.bn_aggr(mv2[:, t, :], stat2[:, t, :])
                last.then_inc(S["ln2_var"], 1)

            per_e = lambda a: a.unsqueeze(2).to_broadcast([P, TPH, E])
            rank = small[:, 0:E].unsqueeze(1).to_broadcast([P, TPH, E])
            top_p, second_p = t1[1], t1[3]
            first, second, masked = t8[2], t8[5], t8[6]
            total, total_eps, kept_sum, kept_rec = t1[5:9]
            row_of, row_1, row_2 = t8[0], t8[1], t8[3]

            def route_start(n):
                first_pick.turn(n)
                logit = ps[:, 7, 0:TPH * E].rearrange("p (t e) -> p t e", e=E)
                dve.wait_ge(S["lg_mm"], n)
                first_pick.link(red(t1[0][:], logit, AX.X, ALU.max))
                tt(lg[:], logit, per_e(t1[0][:]), ALU.subtract).then_inc(S["lg_sub"], 1)


            def route_first(n):
                same, key, top = t8[0], t8[1], t1[2]
                weigh.turn(n)
                dve.wait_ge(S["lg_exp"], n)
                first_pick.did(red(top_p[:], ex[:], AX.X, ALU.max))
                weigh.did(red(total[:], ex[:], AX.X, ALU.add))
                first_pick.due()
                first_pick.did(tt(same[:], ex[:], per_e(top_p[:]), ALU.is_equal))
                weigh.due()
                weigh.did(dve.scalar_tensor_tensor(out=total_eps[:], in0=total[:], scalar=1e-6, in1=top_p[:],
                                                   op0=ALU.mult, op1=ALU.add))
                first_pick.due()
                first_pick.link(tt(key[:], same[:], rank, ALU.mult))
                first_pick.link(red(top[:], key[:], AX.X, ALU.max))
                first_pick.link(tt(first[:], key[:], per_e(top[:]), ALU.is_equal))
                first_pick.link(dve.scalar_tensor_tensor(out=masked[:], in0=first[:], scalar=-4.0, in1=ex[:],
                                                         op0=ALU.mult, op1=ALU.add))

            def route_second(h, n):
                same, key, top = t8[3], t8[4], t1[4]
                second_pick.turn(n)
                second_pick.link(red(second_p[:], masked[:], AX.X, ALU.max))
                second_pick.did(tt(same[:], masked[:], per_e(second_p[:]), ALU.is_equal))
                weigh.due()
                weigh.did(tt(kept_sum[:], total_eps[:], second_p[:], ALU.add))
                second_pick.due()
                second_pick.did(tt(key[:], same[:], rank, ALU.mult))
                weigh.due()
                weigh.did(dve.reciprocal(kept_rec[:], kept_sum[:]))
                second_pick.due()
                second_pick.did(red(top[:], key[:], AX.X, ALU.max))
                weigh.due()
                weigh.did(tt(rowbuf[:, h, 0, :, DIM + 1], top_p[:], kept_rec[:], ALU.mult))
                second_pick.due()
                second_pick.did(tt(second[:], key[:], per_e(top[:]), ALU.is_equal))
                weigh.due()
                weigh.did(tt(rowbuf[:, h, 1, :, DIM + 1], second_p[:], kept_rec[:], ALU.mult))
                second_pick.due()
                tt(chosen[:], first[:], second[:], ALU.add).then_inc(S["chosen_ready"], 1)
                weigh.due()

            counts = ps[:, 7, 64:64 + (TPH + 1) * E].rearrange("p (t e) -> p t e", e=E)

            def places_start(n):
                place.turn(n)
                place.did(tt(base[:], run[:], small[:, E:2 * E], ALU.add))

            def places(h, n):
                dve.wait_ge(S["pos_mm"], n)
                place.due()
                place.did(tt(row_of[:], counts[:, 0:TPH, :], base[:].unsqueeze(1).to_broadcast([P, TPH, E]), ALU.add))
                tt(run[:], counts[:, TPH, :], run[:], ALU.add).then_inc(S["counts_read"], 1)
                place.due()
                place.did(tt(row_1[:], row_of[:], first[:], ALU.mult))
                tt(row_2[:], row_of[:], second[:], ALU.mult).then_inc(S["row_2_ready"], 1)
                place.due()
                place.did(red(slot_f[:, 0, :], row_1[:], AX.X, ALU.add))
                dve.wait_ge(S["row_2_ready"], n)
                place.due()
                place.did(red(slot_f[:, 1, :], row_2[:], AX.X, ALU.add))
                place.due()
                dve.tensor_copy(slots[:, h], slot_f[:]).then_inc(S["slots_ready"], 1)
                dve.wait_ge(S["counts_read"], n)

            def rows_low(j, p):
                dve.wait_ge(S["gT_ev"], j + 1)
                tt(xg_t[:, p, 1, :], ps[:, 2 + p, 0:P], xg_t[:, p, 0, :].bitcast(F32), ALU.subtract)\
                    .then_inc(S["low_ready"], 1)

            def gated(j, p):
                dve.wait_ge(S["g_silu"], j + 1)
                tt(hid[:, p, :], ps[:, p, HIDDEN:2 * HIDDEN], gate[:, p, :], ALU.mult).then_inc(S["h_ready"], 1)

            def hidden_ev(j, p):
                dve.wait_ge(S["hT_mm"], j + 1)
                dve.tensor_copy(hid_t[:, p].rearrange("p c q -> p (c q)"), ps[:, 4 + p, 0:2 * P])\
                    .then_inc(S["hT_ev"], 1)

            def result_ev(j, p, n):
                dve.wait_ge(S["y_mm"], j + 1)
                ts(y_sb[:, n, :], ps[:, 6 + p, 0:DIM], xg[:, n, DIM + 1:ROW], None, ALU.mult).then_inc(S["y_ev"], 1)

            table = Once(dve, "table_link")
            lk = table.link
            le = rows[0:1, 0:E * E].rearrange("o (e f) -> o e f", f=E)
            jj = rows[0:1, E * E:E * E + MOE_TILES * E].rearrange("o (j e) -> o j e", e=E)
            j128 = rows[0:1, E * E + MOE_TILES * E:]

            spread = lambda a, count: a[:].unsqueeze(1).to_broadcast([1, count, E])

            def tiles_up_to():
                return tt(tbe[:], le, tiles[:].unsqueeze(1).to_broadcast([1, E, E]), ALU.mult)

            def list_ends():
                return red(tiles_to[:], tbe[:], AX.X, ALU.add)

            def list_ended(count):
                return tt(ended[:, 0:count, :], spread(tiles_to, count), jj[:, 0:count, :], ALU.is_le)

            def list_jumps(count):
                return tt(jumps[:, 0:count, :], ended[:, 0:count, :], spread(jump, count), ALU.mult)

            def sum_jumps(count):
                return red(tj[0][:, 0:count], jumps[:, 0:count, :], AX.X, ALU.add)

            def add_start(start, count):
                return tt(tj[1][:, 0:count], tj[0][:, 0:count], start, ALU.add)

            def sum_ended(count):
                return red(tj[2][:, 0:count], ended[:, 0:count, :], AX.X, ALU.add)

            def store_list(at, count, done):
                ts(tile_row[:, at:at + count], tj[1][:, 0:count], float(E * REGION), None, ALU.min)
                ts(tile_exp[:, at:at + count], tj[2][:, 0:count], float(E - 1), None, ALU.min).then_inc(done, 1)

            def early_tables():
                dve.wait_ge(S["taken_zeroed"], 1)
                lk(dve.tensor_copy(tb_i[:, 0, :], run[0:1, :]))
                lk(ts(tb_i[:, 1, :], tb_i[:, 0, :], 7, None, ALU.arith_shift_right))
                lk(dve.tensor_copy(tiles[:], tb_i[:, 1, :]))
                lk(ts(jump[:], tiles[:], -float(P), float(REGION), ALU.mult, ALU.add))
                lk(tiles_up_to())
                lk(list_ends())
                lk(list_ended(EARLY))
                table.did(list_jumps(EARLY))
                table.did(sum_ended(EARLY))
                table.due()
                lk(sum_jumps(EARLY))
                lk(add_start(j128[:, 0:EARLY], EARLY))
                store_list(0, EARLY, S["early_tables"])

            def early_taken():
                lk(tt(tb[0][:], tiles[:], tiles_to[:], ALU.subtract))
                lk(ts(tb[1][:], tb[0][:], float(EARLY), 0.0, ALU.add, ALU.max))
                lk(tt(taken[:, 0:E], tb[1][:], tiles[:], ALU.min))
                lk(ts(tb[2][:], taken[:, 0:E], float(P), None, ALU.mult))
                lk(tt(late_start[:], j128[:, 0:LATE], tb[2][:, 0:1].to_broadcast([1, LATE]), ALU.add))

            def late_counts(part):
                if part == 0:
                    table.did(tt(tb[0][:], run[0:1, :], small[0:1, E:2 * E], ALU.add))
                    table.did(ts(tb_i[:, 0, :], run[0:1, :], float(P - 1), None, ALU.add))
                elif part == 1:
                    table.due()
                    dve.tensor_copy(pad_at[:], tb[0][:]).then_inc(S["pads_known"], 1)
                    table.did(ts(tb_i[:, 1, :], tb_i[:, 0, :], 7, None, ALU.arith_shift_right))
                elif part == 2:
                    table.due()
                    lk(dve.tensor_copy(tb[1][:], tb_i[:, 1, :]))
                    table.did(dve.scalar_tensor_tensor(out=tb[2][:], in0=tb[1][:], scalar=-1.0, in1=taken[:, 1:],
                                                       op0=ALU.mult, op1=ALU.add))
                    table.did(tt(tiles[:], tb[1][:], taken[:, 0:E], ALU.subtract))
                elif part == 3:
                    table.due()
                    table.did(ts(jump[:], tb[2][:], float(P), float(REGION), ALU.mult, ALU.add))
                    table.did(tiles_up_to())

            def late_list(part):
                table.due()
                if part == 0:
                    table.did(list_ends())
                elif part == 1:
                    table.did(list_ended(LATE))
                elif part == 2:
                    table.did(list_jumps(LATE))
                elif part == 3:
                    table.did(sum_jumps(LATE))
                elif part == 4:
                    table.did(add_start(late_start[:], LATE))
                    table.did(sum_ended(LATE))
                elif part == 5:
                    store_list(EARLY, LATE, S["tables"])

            def step(i, h, before, n, after):
                softmax_a(n)
                if not last_pair(i):
                    stats(h, i // 2 + 2, kept(dve, i + 3))
                softmax_b(n)
                if after is not None:
                    rotate_parts(1 - h, after, 0, S["q_mm"], S["q_read"])
                    rotate_parts(1 - h, after, 1, S["k_mm"], S["k_read"])
                if before is not None:
                    route_start(before)
                if after is not None:
                    rotate_k(1 - h, after)
                if before is not None:
                    route_first(before)
                if after is None:
                    route_second(1 - h, before)
                    early_tables()
                sum_x2(h, n)
                if before is not None:
                    if after is not None:
                        route_second(1 - h, before)
                    places_start(before)
                    places(1 - h, before)
                if after is None:
                    rows_low(0, 0)
                    rows_low(1, 1)
                    early_taken()

            def front(h, n):
                dve.wait_ge(S["consts"], CONSTS)
                rotate_parts(h, n, 0, S["q_mm"], S["q_read"])
                rotate_parts(h, n, 1, S["k_mm"], S["k_read"])
                rotate_k(h, n)

            dve.sem_inc(S["x2_free"], 2)
            dve.memset(xn_t[:, 0:BLOCK], 0.0).then_inc(S["halo"], 1)
            dve.memset(k_t[:, 0:BLOCK], 0.0).then_inc(S["halo"], 1)
            dve.memset(taken[:], 0.0).then_inc(S["taken_zeroed"], 1)
            stats(0, 1, 1)
            stats(1, 1, 2)
            dve.wait_ge(S["zeroed"], 2)
            run_halves(dve, front, step)

            route_start(HALVES)
            route_first(HALVES)
            route_second(1, HALVES)
            places_start(HALVES)
            gated(0, 0)
            rows_low(2, 0)
            places(1, HALVES)

            def turn(j):
                if j >= 2 and j + 1 < MOE_TILES:
                    rows_low(j + 1, (j + 1) % 2)
                if j >= 1:
                    hidden_ev(j - 1, (j - 1) % 2)
                gated(j, j % 2)
                if j >= 2:
                    result_ev(j - 2, j % 2, (j - 2) % XB)

            first = 2 + XB
            late_counts(0)
            for j in range(1, first):
                turn(j)
                if j < 4:
                    late_counts(j)
                elif j < 10:
                    late_list(j - 4)
            full = (MOE_TILES - first) // XB
            with dve.Fori(0, full) as m:
                for n in range(XB):
                    j = m * XB + first + n
                    rows_low(j + 1, 1 - n % 2)
                    hidden_ev(j - 1, 1 - n % 2)
                    gated(j, n % 2)
                    result_ev(j - 2, n % 2, n)
            for j in range(first + full * XB, MOE_TILES):
                turn(j)
            j = MOE_TILES
            hidden_ev(j - 1, (j - 1) % 2)
            result_ev(j - 2, j % 2, (j - 2) % XB)
            result_ev(j - 1, (j - 1) % 2, (j - 1) % XB)

            dve.wait_ge(x2_stored[0], 16 * (HALVES // 2))
            dve.wait_ge(x2_stored[1], 16 * (HALVES // 2))
            for b in range(BATCH):
                dve.wait_ge(res_loaded[b], 16)
                for part in range(2):
                    tile = x2_all[:, b * TPB + part * TPH:b * TPB + (part + 1) * TPH, :]
                    t = slice(part * TPH, (part + 1) * TPH)
                    tt(tile, tile, res[:, b, t, 0, :], ALU.add).then_inc(S["half_summed"], 1)
                    dve.wait_ge(S["half_summed"], 2 * b + part + 1)
                    tt(tile, tile, res[:, b, t, 1, :], ALU.add).then_inc(S["summed"], 1)


def _tables():
    inv = (1.0 / np.float32(10000.0) ** (np.arange(0, HEAD, 2, dtype=np.float32) / np.float32(HEAD))).astype(np.float32)
    angle = (np.arange(SEQ, dtype=np.float32)[None, :] * inv[:, None]).astype(np.float32)
    cos = np.tile(np.cos(angle), (4, 1)).astype(np.float32)
    sin = np.sin(angle).astype(np.float32)
    sin = np.tile(np.concatenate([-sin, sin]), (2, 1)).astype(np.float32)
    k, m = np.arange(P)[:, None], np.arange(P)[None, :]
    q, key = np.arange(P)[:, None], np.arange(64)[None, :] - BLOCK
    dist = q % BLOCK - key
    seen = (dist >= 0) & (dist < BLOCK)
    start = seen & ((q >= BLOCK) | (key >= 0))
    mask = np.concatenate([np.where(s, 0.0, MASKED) for s in (start, seen)], axis=1)
    squares = np.concatenate([k == m, k < m, np.ones((P, P)), mask], axis=1).astype(np.float32)
    e = np.arange(EXPERTS)
    small = np.tile(np.concatenate([EXPERTS - e, e * REGION]).astype(np.float32), (P, 1))
    j = np.arange(MOE_TILES)
    row = np.concatenate([(e[None, :] <= e[:, None]).ravel(), np.repeat(j, EXPERTS), j * P]).astype(np.float32)
    return {"cos": cos, "sin": sin, "ident": (k == m).astype(np.float32), "small": small,
            "row": row[None, :], "squares": squares}


def kernel(L0_attn_x, L0_attn_ln_w, L0_attn_ln_b, L0_attn_w_qkv, L0_attn_w_out, L0_ffn_router_w,
           L0_ffn_w13, L0_ffn_w2):
    import concourse.bacc as bacc
    from concourse.bass_utils import run_bass_kernel_spmd

    qkv_t = np.asarray(L0_attn_w_qkv).T
    swap = np.arange(2 * DIM).reshape(-1, 2, HEAD // 2)[:, ::-1].ravel()
    arrays = {
        "x": L0_attn_x, "ln_w": np.asarray(L0_attn_ln_w)[:, None], "ln_b": np.asarray(L0_attn_ln_b)[:, None],
        "w_qk_t": qkv_t[:, :2 * DIM], "w_rot_t": qkv_t[:, swap], "w_v": np.asarray(L0_attn_w_qkv)[2 * DIM:],
        "w_out_t": np.asarray(L0_attn_w_out).T,
        "router_t": np.asarray(L0_ffn_router_w).T, "w13": L0_ffn_w13, "w2": L0_ffn_w2, **_tables(),
    }
    arrays = {n: np.ascontiguousarray(a) for n, a in arrays.items()}
    nc = bacc.Bacc("TRN2", target_bir_lowering=False, num_devices=1)
    args = [nc.dram_tensor(f"in_{n}", a.shape, mybir.dt.from_np(a.dtype), kind="ExternalInput").ap()
            for n, a in arrays.items()]
    args.append(nc.dram_tensor("out", (BATCH, SEQ, DIM), mybir.dt.float32, kind="ExternalOutput").ap())
    program(nc, *args)
    r = run_bass_kernel_spmd(nc, [{f"in_{n}": a for n, a in arrays.items()}], core_ids=[0])
    return r.results[0]["out"]
```
